# Optimizing a Trainium2 kernel written in Bass

```python
import numpy as np
import jax
import jax.numpy as jnp

def _softmax(x, axis=-1):
    return jax.nn.softmax(x, axis=axis)

def _gelu(x):
    return jax.nn.gelu(x, approximate=True)

def _silu(x):
    return jax.nn.silu(x)

def _sigmoid(x):
    return jax.nn.sigmoid(x)

def _layernorm(x, axis=-1, eps=1e-05):
    m = jnp.mean(x, axis=axis, keepdims=True)
    v = jnp.var(x, axis=axis, keepdims=True)
    return (x - m) / jnp.sqrt(v + eps)

def _scatter_add(tgt, idx, src, axis=0):
    return tgt.at[idx].add(src)

def _segment_sum(src, seg, n):
    return jax.ops.segment_sum(src, seg, n)
kernel_name = 'mk_adj_resnorm_d2_adj_r2_cf958c'

def setup_inputs(seed: int=0):
    np.random.seed(seed)
    _w = jnp.asarray

    def _rec_inputs():
        import jax
        import jax.numpy as jnp
        _gk = jax.random.key(seed)
        x = 0.0001732 + 1 * jax.random.normal(jax.random.fold_in(_gk, 1), (5120, 64), jnp.float32)
        _a = jax.random.bernoulli(jax.random.fold_in(_gk, 2), 0.0015625, (5120, 5120))
        _af = _a.astype(jnp.float32)
        _af = _af * jax.random.uniform(jax.random.fold_in(_gk, 3), (5120, 5120), jnp.float32, 0.05, 0.02)
        adj = _af
        return (x, adj)
    x, adj = _rec_inputs()

    def _L0_gnn_setup():
        import jax, jax.numpy as jnp
        import numpy as np
        N_USERS = 2048
        N_ITEMS = 3072
        EMB = 64
        LN_EPS = 1e-05
        key = jax.random.key(seed)
        ks = jax.random.split(key, 10)
        N = N_USERS + N_ITEMS
        ego = jax.random.normal(ks[0], (N, EMB), jnp.float32)
        adj = (jax.random.uniform(ks[1], (N, N), jnp.float32) < 0.01).astype(jnp.float32) * 0.02
        xav = float(np.sqrt(6.0 / (EMB + EMB)))
        W_u = jax.random.uniform(ks[2], (EMB, EMB), jnp.float32, -xav, xav)
        W_i = jax.random.uniform(ks[3], (EMB, EMB), jnp.float32, -xav, xav)
        diag_u = jax.random.uniform(ks[4], (N_USERS,), jnp.float32, 0.99, 1.01)
        diag_i = jax.random.uniform(ks[5], (N_ITEMS,), jnp.float32, 0.99, 1.01)
        par_u = jax.random.uniform(ks[6], (2,), jnp.float32, 0.0, 0.99)
        par_i = jax.random.uniform(ks[7], (2,), jnp.float32, 0.0, 0.99)
        ln_gamma = jnp.ones((EMB,), jnp.float32)
        ln_beta = jnp.zeros((EMB,), jnp.float32)
        return {'ego_embeddings': ego, 'adj': adj, 'W_u': W_u, 'diag_u': diag_u, 'par_u': par_u, 'W_i': W_i, 'diag_i': diag_i, 'par_i': par_i, 'ln_gamma': ln_gamma, 'ln_beta': ln_beta}
    _L0_gnn_all = _L0_gnn_setup()
    _L0_gnn_in = {k: v for k, v in _L0_gnn_all.items() if k in ('W_u', 'diag_u', 'par_u', 'W_i', 'diag_i', 'par_i', 'ln_gamma', 'ln_beta')}
    del _L0_gnn_all

    def _L1_gnn_setup():
        import jax, jax.numpy as jnp
        import numpy as np
        N = 2048
        D = 64
        NUM_LAYERS = 2
        THETA0 = 0.000244
        THETA_MAX = 0.0003
        LAM = 0.1
        TAU = 1.0
        EPS = 1e-06
        H_DENSITY = 0.005

        def _safe_norm(x, axis):
            return jnp.sqrt(jnp.maximum(jnp.sum(x * x, axis=axis), 1e-16))

        def _layer(x, H, W, Theta, Wq, bq, Wv, bv, iteration):
            scale = D ** (-0.5)
            theta_base = THETA0 + (1.0 - np.exp(-LAM * iteration)) * (THETA_MAX - THETA0)
            th_comp = theta_base
            th_edge = min(theta_base, 0.8)
            th_node = min(theta_base, 0.7)
            structural = _safe_norm(x @ W, axis=1)
            Q = x @ Wq + bq
            V = x @ Wv + bv
            edge_feat = H.T @ V
            att = Q @ edge_feat.T * scale * H
            att = jax.nn.softmax(att, axis=1)
            att_scores = att.mean(axis=0)
            importance = 0.5 * structural + 0.5 * att_scores
            comp_scores = jax.nn.softmax(importance / TAU)
            comp_mask = comp_scores >= th_comp
            x_comp = x * comp_mask[:, None]
            nrm = jnp.maximum(_safe_norm(x_comp, axis=1), 1e-08)
            xn = x_comp / nrm[:, None]
            cos = xn @ xn.T
            edge_scores = jax.nn.softmax(cos * H / TAU, axis=1)
            edge_mask = (edge_scores >= th_edge) & comp_mask[:, None]
            H_pruned = H * edge_mask
            connectivity = H_pruned.sum(axis=1)
            feat_mag = _safe_norm(x_comp, axis=1)
            node_scores = jax.nn.softmax(connectivity * feat_mag / TAU)
            connected = (H_pruned * edge_mask).sum(axis=1) > 0
            node_mask = (node_scores >= th_node) & connected
            x_final = x_comp * node_mask[:, None]
            vdeg = jnp.maximum(H_pruned.sum(axis=1), EPS)
            edeg = jnp.maximum(H_pruned.sum(axis=0), EPS)
            dv_isqrt = 1.0 / jnp.sqrt(vdeg)
            de_inv = 1.0 / edeg
            transformed = x_final @ W
            agg = H_pruned.T * dv_isqrt[None, :] @ transformed
            agg = agg * de_inv[:, None]
            msg = dv_isqrt[:, None] * (H_pruned @ agg)
            msg = msg @ Theta
            return jax.nn.relu(msg)
        key = jax.random.key(seed)
        ks = jax.random.split(key, 8)
        xav = 0.125
        X = jax.random.normal(ks[0], (N, D), jnp.float32) * 0.05
        W = jax.random.normal(ks[1], (D, D), jnp.float32) * xav
        Theta = jax.random.normal(ks[2], (D, D), jnp.float32) * xav
        Wq = jax.random.normal(ks[3], (D, D), jnp.float32) * xav
        bq = jnp.zeros((D,), jnp.float32)
        Wv = jax.random.normal(ks[4], (D, D), jnp.float32) * xav
        bv = jnp.zeros((D,), jnp.float32)
        H = (jax.random.uniform(ks[7], (N, N)) < H_DENSITY).astype(jnp.float32)
        return {'X': X, 'W': W, 'Theta': Theta, 'Wq': Wq, 'bq': bq, 'Wv': Wv, 'bv': bv, 'H': H}
    _L1_gnn_all = _L1_gnn_setup()
    _L1_gnn_in = {k: v for k, v in _L1_gnn_all.items() if k in ('W', 'Theta', 'Wq', 'bq', 'Wv', 'bv')}
    del _L1_gnn_all
    return {'x': x, 'adj': adj, 'L0_gnn_W_u': _L0_gnn_in['W_u'], 'L0_gnn_diag_u': _L0_gnn_in['diag_u'], 'L0_gnn_par_u': _L0_gnn_in['par_u'], 'L0_gnn_W_i': _L0_gnn_in['W_i'], 'L0_gnn_diag_i': _L0_gnn_in['diag_i'], 'L0_gnn_par_i': _L0_gnn_in['par_i'], 'L0_gnn_ln_gamma': _L0_gnn_in['ln_gamma'], 'L0_gnn_ln_beta': _L0_gnn_in['ln_beta'], 'L1_gnn_W': _L1_gnn_in['W'], 'L1_gnn_Theta': _L1_gnn_in['Theta'], 'L1_gnn_Wq': _L1_gnn_in['Wq'], 'L1_gnn_bq': _L1_gnn_in['bq'], 'L1_gnn_Wv': _L1_gnn_in['Wv'], 'L1_gnn_bv': _L1_gnn_in['bv']}

def reference(x, adj, L0_gnn_W_u, L0_gnn_diag_u, L0_gnn_par_u, L0_gnn_W_i, L0_gnn_diag_i, L0_gnn_par_i, L0_gnn_ln_gamma, L0_gnn_ln_beta, L1_gnn_W, L1_gnn_Theta, L1_gnn_Wq, L1_gnn_bq, L1_gnn_Wv, L1_gnn_bv):
    import jax
    import jax.numpy as jnp

    def _L0_gnn_ref(ego_embeddings, adj, W_u, diag_u, par_u, W_i, diag_i, par_i, ln_gamma, ln_beta):
        import jax, jax.numpy as jnp
        import numpy as np
        N_USERS = 2048
        N_ITEMS = 3072
        EMB = 64
        LN_EPS = 1e-05
        nu = diag_u.shape[0]
        res = ego_embeddings
        ego_u = ego_embeddings[:nu]
        ego_i = ego_embeddings[nu:]
        u = par_u[0] * par_u[1] * (diag_u[:, None] * ego_u @ W_u) + ego_u
        i = par_i[0] * par_i[1] * (diag_i[:, None] * ego_i @ W_i) + ego_i
        e = jnp.concatenate([u, i], axis=0)
        h = adj @ (adj.T @ e)
        mu = jnp.mean(h, axis=-1, keepdims=True)
        var = jnp.var(h, axis=-1, keepdims=True)
        out = (h - mu) * jax.lax.rsqrt(var + LN_EPS) * ln_gamma + ln_beta + res
        return out

    def _L1_gnn_ref(X, W, Theta, Wq, bq, Wv, bv, H):
        import jax, jax.numpy as jnp
        import numpy as np
        N = 2048
        D = 64
        NUM_LAYERS = 2
        THETA0 = 0.000244
        THETA_MAX = 0.0003
        LAM = 0.1
        TAU = 1.0
        EPS = 1e-06
        H_DENSITY = 0.005

        def _safe_norm(x, axis):
            return jnp.sqrt(jnp.maximum(jnp.sum(x * x, axis=axis), 1e-16))

        def _layer(x, H, W, Theta, Wq, bq, Wv, bv, iteration):
            scale = D ** (-0.5)
            theta_base = THETA0 + (1.0 - np.exp(-LAM * iteration)) * (THETA_MAX - THETA0)
            th_comp = theta_base
            th_edge = min(theta_base, 0.8)
            th_node = min(theta_base, 0.7)
            structural = _safe_norm(x @ W, axis=1)
            Q = x @ Wq + bq
            V = x @ Wv + bv
            edge_feat = H.T @ V
            att = Q @ edge_feat.T * scale * H
            att = jax.nn.softmax(att, axis=1)
            att_scores = att.mean(axis=0)
            importance = 0.5 * structural + 0.5 * att_scores
            comp_scores = jax.nn.softmax(importance / TAU)
            comp_mask = comp_scores >= th_comp
            x_comp = x * comp_mask[:, None]
            nrm = jnp.maximum(_safe_norm(x_comp, axis=1), 1e-08)
            xn = x_comp / nrm[:, None]
            cos = xn @ xn.T
            edge_scores = jax.nn.softmax(cos * H / TAU, axis=1)
            edge_mask = (edge_scores >= th_edge) & comp_mask[:, None]
            H_pruned = H * edge_mask
            connectivity = H_pruned.sum(axis=1)
            feat_mag = _safe_norm(x_comp, axis=1)
            node_scores = jax.nn.softmax(connectivity * feat_mag / TAU)
            connected = (H_pruned * edge_mask).sum(axis=1) > 0
            node_mask = (node_scores >= th_node) & connected
            x_final = x_comp * node_mask[:, None]
            vdeg = jnp.maximum(H_pruned.sum(axis=1), EPS)
            edeg = jnp.maximum(H_pruned.sum(axis=0), EPS)
            dv_isqrt = 1.0 / jnp.sqrt(vdeg)
            de_inv = 1.0 / edeg
            transformed = x_final @ W
            agg = H_pruned.T * dv_isqrt[None, :] @ transformed
            agg = agg * de_inv[:, None]
            msg = dv_isqrt[:, None] * (H_pruned @ agg)
            msg = msg @ Theta
            return jax.nn.relu(msg)
        x = X
        for it in range(NUM_LAYERS):
            x = _layer(x, H, W, Theta, Wq, bq, Wv, bv, it)
        return x
    x = _layernorm(x + _L0_gnn_ref(x, adj, L0_gnn_W_u, L0_gnn_diag_u, L0_gnn_par_u, L0_gnn_W_i, L0_gnn_diag_i, L0_gnn_par_i, L0_gnn_ln_gamma, L0_gnn_ln_beta), axis=-1)
    x = _layernorm(x + _L1_gnn_ref(x, L1_gnn_W, L1_gnn_Theta, L1_gnn_Wq, L1_gnn_bq, L1_gnn_Wv, L1_gnn_bv, adj), axis=-1)
    return x

_drawn_inputs = setup_inputs


def setup_inputs(seed=0):
    import zlib

    import numpy as np

    out = dict(_drawn_inputs(seed))
    spreads = {'L0_gnn_ln_gamma': (1.0, 0.2),
     'L0_gnn_ln_beta': (0.0, 0.1),
     'L1_gnn_bq': (0.0, 0.1),
     'L1_gnn_bv': (0.0, 0.1)}
    factors = {'L0_gnn_diag_u': 8.0, 'L0_gnn_W_i': 6.105, 'L0_gnn_diag_i': 8.0}
    for name, (base, spread) in spreads.items():
        noise = np.random.default_rng([zlib.crc32(name.encode()), seed]).standard_normal(out[name].shape)
        drawn = base * np.exp(spread * noise) if base else spread * noise
        out[name] = jnp.asarray(drawn.astype(out[name].dtype))
    for name, factor in factors.items():
        out[name] = (out[name] * factor).astype(out[name].dtype)
    return out
```

```python
import math
from contextlib import ExitStack

import concourse.bass as bass
from concourse import mybir



def adjacency_layers_kernel(nc, x, x_t, adj, w_ui, diag, par, gamma, beta,
                            w_qv, w_q, theta, b_q, b_v, out):
    f32 = mybir.dt.float32
    bf16 = mybir.dt.bfloat16
    i32 = mybir.dt.int32
    ALU = mybir.AluOpType
    ACT = mybir.ActivationFunctionType
    X = mybir.AxisListType.X

    P = 128
    N, D = x.shape
    T = N // P
    USER_TILES = 2048 // P
    CH = 512
    BANKS = N // (2 * CH)
    HALF = N // 2
    RING = 4
    QUADS = 4
    QCOLS = N // QUADS
    BLOCKS = QCOLS // 32
    CUTS = 4
    BPT = BLOCKS // CUTS
    GROUP = 512
    GROUPS = N // GROUP
    TPG = GROUP // P
    RSUB = GROUP // 32
    LN_EPS = 1e-5
    DEG_EPS = 1e-6
    SCALE = float(D) ** -0.5
    ROUNDS = 2
    THETA = [0.000244 + (1.0 - math.exp(-0.1 * it)) * (0.0003 - 0.000244) for it in range(ROUNDS)]
    LIMIT = 0.5 * math.log(N * THETA[0]) - 0.01

    pruned = nc.dram_tensor("pruned_adjacency", [N, N], f32, kind="Internal").ap()

    ctx = ExitStack()
    with ctx:
        def sb(name, shape, dt=f32):
            return ctx.enter_context(nc.sbuf_tensor(name, shape, dt))

        def sem(name):
            return ctx.enter_context(nc.semaphore(name))

        ring = [sb(f"ring{s}", [P, N]) for s in range(RING)]
        turned = [sb(f"turned{s}", [P, N]) for s in range(2)]
        x_all = sb("x_all", [P, T, D])
        x1_all = sb("x1_all", [P, T, D])
        rows_in = sb("rows_in", [P, T, D])
        cols_t = sb("cols_t", [P, HALF])
        cols = sb("cols", [P, BLOCKS, D])
        staged = [sb(f"staged{s}", [P, D]) for s in range(RING)]
        sums = [sb(f"sums{s}", [P, GROUP]) for s in range(2)]
        ident = sb("ident", [P, P])
        stack = sb("stack", [P, D])
        zeros = sb("zeros", [P, CH], bf16)
        w_ui_sb = sb("w_ui_sb", [D, 2 * D])
        diag_sb = sb("diag_sb", [P, T])
        par_sb = sb("par_sb", [P, 4])
        pp = sb("pp", [P, 2])
        gamma_sb = sb("gamma_sb", [P, D])
        beta_sb = sb("beta_sb", [P, D])
        row_max = sb("row_max", [P, T])
        part_max = sb("part_max", [P, 1])
        all_max = sb("all_max", [P, 1])
        flag = sb("flag", [P, 1], i32)
        ln_h = sb("ln_h", [P, TPG, D])
        ln_c = sb("ln_c", [P, TPG, D])
        ln_sq = sb("ln_sq", [P, TPG, D])
        ln_y = sb("ln_y", [P, TPG, D])
        ln_sum = sb("ln_sum", [P, TPG])
        ln_mean = sb("ln_mean", [P, TPG])
        ln_var = sb("ln_var", [P, TPG])
        ln_rstd = sb("ln_rstd", [P, TPG])
        ln_out = sb("ln_out", [P, TPG, D])
        ln_x = sb("ln_x", [P, TPG, D])
        minus_half = sb("minus_half", [P, TPG])
        inv_d = sb("inv_d", [P, TPG])
        neg_inv_d = sb("neg_inv_d", [P, TPG])
        eps_tile = sb("eps_tile", [P, TPG])
        w_qv_sb = sb("w_qv_sb", [D, 2 * D])
        w_q_sb = sb("w_q_sb", [D, D])
        theta2 = sb("theta2", [P, D])
        b_q_sb = sb("b_q_sb", [D, 1])
        b_v_sb = sb("b_v_sb", [P, D])
        thresholds = sb("thresholds", [P, ROUNDS])
        threshold = sb("threshold", [P, 1])
        x_pad = sb("x_pad", [P, P])
        xt_tile = sb("xt_tile", [D, P])
        ones = sb("ones", [P, P])
        node_a, node_b, node_c = (sb(f"node_{k}", [P, T]) for k in "abc")
        att = sb("att", [P, T])
        comp_mask = sb("comp_mask", [P, T])
        feat_mag = sb("feat_mag", [P, T])
        conn = sb("conn", [P, T])
        edge_deg = sb("edge_deg", [P, BLOCKS])
        dv = sb("dv", [P, T])
        part = sb("part", [P, 1])
        neg_max = sb("neg_max", [P, 1])
        part_sum = sb("part_sum", [P, 1])
        recip = sb("recip", [P, 1])
        diagonal = sb("diagonal", [P, P])
        mask_tile = sb("mask_tile", [P, 1])
        conn_tile = sb("conn_tile", [P, 1])

        xt_all = turned[0][0:D, :]
        edge_t = turned[1][0:D, :]
        h_rows, logits = ring[0], ring[1]
        tmp = ring[2][:, 0:T * D].rearrange("p (t d) -> p t d", d=D)
        xw_all = cols

        bank = [ctx.enter_context(nc.psum_tensor(f"bank{b}", [P, CH], f32)) for b in range(8)]
        sum_bank = [bank[5], bank[6]]
        nat_bank = bank[7]

        const_loaded = sem("const_loaded")
        const_made = sem("const_made")
        zeros_made = sem("zeros_made")
        ident_clear = sem("ident_clear")
        pp_made = sem("pp_made")
        xw_done = sem("xw_done")
        e_scaled = sem("e_scaled")
        e_made = sem("e_made")
        rows_loaded = [sem(f"rows_loaded{s}") for s in range(RING)]
        tile_staged = sem("tile_staged")
        rows_used = sem("rows_used")
        rows_scanned = sem("rows_scanned")
        cols_copied = sem("cols_copied")
        cols_turned = sem("cols_turned")
        cols_ready = sem("cols_ready")
        tiles_loaded = [sem(f"tiles_loaded{s}") for s in range(RING)]
        tiles_turned = sem("tiles_turned")
        tiles_used = sem("tiles_used")
        sums_copied = sem("sums_copied")
        nat_ready = sem("nat_ready")
        nat_read = sem("nat_read")
        ln_sums = sem("ln_sums")
        ln_steps = sem("ln_steps")
        ln_stored = sem("ln_stored")
        max_found = sem("max_found")
        flag_made = sem("flag_made")
        weights_loaded = sem("weights_loaded")
        gate = sem("gate")
        passed = sem("passed")
        x_staged = sem("x_staged")
        x_turned = sem("x_turned")
        xt_ready = sem("xt_ready")
        projected = sem("projected")
        q_kept = sem("q_kept")
        h_loaded = sem("h_loaded")
        row_staged = sem("row_staged")
        chunk_scored = sem("chunk_scored")
        chunk_masked = sem("chunk_masked")
        max_ready = sem("max_ready")
        exp_ready = sem("exp_ready")
        recip_ready = sem("recip_ready")
        edges_kept = sem("edges_kept")
        pruned_made = sem("pruned_made")
        pruned_stored = sem("pruned_stored")
        row_folded = sem("row_folded")
        node_steps = sem("node_steps")
        mask_staged = sem("mask_staged")
        row_kept = sem("row_kept")
        row_added = sem("row_added")
        msg_kept = sem("msg_kept")
        msg_added = sem("msg_added")
        small_loaded = sem("small_loaded")

        block = ctx.enter_context(nc.Block())

        def half(h):
            return slice(D * h, D * h + D)

        def turned_block(t, b):
            return turned[t][:, CH * b:CH * b + CH]

        def perm(ap, b):
            return ap.rearrange("p (a b c) -> p b a c", a=QUADS, b=BLOCKS)[:, b]


        def load_rows(sp, src, call, it, first=False):
            for s in range(RING):
                n = it * RING + s
                if not first:
                    sp.wait_ge(rows_used, n + (call * T + 1 - RING))
                    if call is L0:
                        sp.wait_ge(rows_scanned, n + (1 - RING))
                sp.dma_start(ring[s][:, :], src[bass.ds(n * P, P), :]).then_inc(rows_loaded[s], 16)

        def stage_rows(act, call, it, first=False):
            for s in range(RING):
                n = it * RING + s
                if not first:
                    act.wait_ge(rows_used, n + (call * T + 1 - RING))
                act.copy(staged[s][:, :], rows_in[:, bass.ds(n, 1), :]).then_inc(tile_staged, 1)

        def multiply_rows(pe, call, it):
            for s in range(RING):
                n = it * RING + s
                pe.wait_ge(rows_loaded[s], (call * (T // RING) + it + 1) * 16)
                pe.wait_ge(tile_staged, n + (call * T + 1))
                for b in range(BANKS):
                    for h in range(2):
                        mm = pe.matmul(bank[b][half(h), :], staged[s][:, :],
                                       ring[s][:, HALF * h + CH * b:HALF * h + CH * b + CH],
                                       start=False, stop=False, skip_group_check=True)
                mm.then_inc(rows_used, 1)

        def clear_sums(pe):
            for b in range(BANKS):
                for h in range(2):
                    mm = pe.matmul(bank[b][half(h), :], zeros[:, 0:D], zeros[:, :],
                                   start=True, stop=False, skip_group_check=True)

        def copy_cols(act, b):
            to = cols_t[:, :].rearrange("p (b a c) -> p a b c", a=2, b=BLOCKS)
            first, last = b * CH // 32, (b + 1) * CH // 32
            for a in range(2):
                lo, hi = max(first, a * BLOCKS), min(last, (a + 1) * BLOCKS)
                if lo < hi:
                    at = bank[b][:, 32 * (lo - first):32 * (hi - first)].rearrange("p (b c) -> p b c", c=32)
                    copied = act.copy(to[:, a, lo - a * BLOCKS:hi - a * BLOCKS, :], at)
            copied.then_inc(cols_copied, 1)

        def turn_cols(pe, use):
            pe.wait_ge(cols_copied, use * BANKS + BANKS)
            pe.sem_inc(passed, 1)
            for b in range(BLOCKS):
                for h in range(2):
                    src = cols_t[half(h), D * b:D * b + D]
                    mm = pe.matmul(bank[b // 8][half(h), D * (b % 8):D * (b % 8) + D], src,
                                   ident[half(h), half(h)], start=True, stop=True)
                if b % 8 == 7:
                    mm.then_inc(cols_turned, 1)

        def load_tiles(sp, src, call, it, units, first=False):
            for u in units:
                n = it * (2 * CUTS) + u
                s = u % RING
                g, q = it * 2 + u // CUTS, u % CUTS
                if first:
                    sp.wait_ge(rows_used, T - RING + 1 + s)
                    sp.wait_ge(rows_scanned, T - RING + 1 + s)
                else:
                    sp.wait_ge(tiles_turned, n + (call * (GROUPS * CUTS) + 1 - RING))
                dst = ring[s][:, :].rearrange("p (R k) -> p R k", R=RSUB)
                for a in range(QUADS):
                    c0 = QCOLS * a + q * BPT * 32
                    piece = src[bass.ds(g * GROUP, GROUP), c0:c0 + BPT * 32]
                    sp.dma_start(dst[32 * a:32 * a + 32],
                                 piece.rearrange("(R r) k -> r R k", r=32)).then_inc(tiles_loaded[s], 16)

        def turn_tiles(dve, call, it, units, first=False):
            for u in units:
                n = it * (2 * CUTS) + u
                s = u % RING
                dve.wait_ge(tiles_loaded[s], (call * (GROUPS * CUTS // RING) + it * 2 + u // RING + 1) * 64)
                if not first:
                    dve.wait_ge(tiles_used, n + (call * (GROUPS * CUTS) - 1))
                nc.vector.transpose(
                    turned[u % 2][:, :].rearrange("p (b R r) -> p R b r", b=BPT, R=RSUB),
                    ring[s][:, :].rearrange("p (R b c) -> p R b c", R=RSUB, b=BPT),
                ).then_inc(tiles_turned, 1)

        def multiply_tiles(pe, call, it, closing):
            for u in range(2 * CUTS):
                n = it * (2 * CUTS) + u
                k, q = u // CUTS, u % CUTS
                pe.wait_ge(tiles_turned, n + (call * (GROUPS * CUTS) + 1))
                for j in range(BPT):
                    mm = pe.matmul(sum_bank[k][half(j % 2), :], cols[:, q * BPT + j, :],
                                   turned_block(u % 2, j), start=(q == 0 and j < 2),
                                   stop=(q == CUTS - 1 and j >= BPT - 2))
                mm.then_inc(tiles_used, 1)
                if q == CUTS - 1:
                    g = it * 2 + k
                    pe.wait_ge(sums_copied, g + (call * GROUPS + 1))
                    pe.wait_ge(nat_read, g + (call * GROUPS + 1))
                    for t in range(TPG):
                        mm = pe.matmul(nat_bank[:, D * t:D * t + D], sums[k][:, P * t:P * t + P],
                                       closing[:, :], start=True, stop=True)
                    mm.then_inc(nat_ready, 1)

        def copy_sums(act, call, it, k):
            g = it * 2 + k
            act.wait_ge(tiles_used, (g + (call * GROUPS + 1)) * CUTS)
            act.copy(sums[k][:, :], sum_bank[k][:, :]).then_inc(sums_copied, 1)

        LN_STEPS = 6

        def sum_features(act, src):
            for t in range(TPG):
                last = nc.scalar.activation(ln_sq[:, t, :], src[:, t, :], ACT.Copy,
                                            accum_out=ln_sum[:, t:t + 1])
            last.then_inc(ln_sums, 1)

        def sum_squares(act):
            for t in range(TPG):
                last = nc.scalar.activation(ln_sq[:, t, :], ln_c[:, t, :], ACT.Square,
                                            accum_out=ln_sum[:, t:t + 1])
            last.then_inc(ln_sums, 1)

        def store_group(act, g):
            act.dma_start(out.rearrange("(g t p) d -> g p t d", p=P, t=TPG)[bass.ds(g, 1)].squeeze(0),
                          ln_out[:, :, :]).then_inc(ln_stored, 16)

        def spread(ap):
            return ap.unsqueeze(2).to_broadcast([P, TPG, D])

        def over_tiles(ap):
            return ap.unsqueeze(1).to_broadcast([P, TPG, D])

        L0 = 0
        SUMS0, STEPS0 = 6, 3 * LN_STEPS + 4
        SUMS1, STEPS1 = 2, LN_STEPS

        class Steps:

            def __init__(self, pool, base):
                self.pool, self.base, self.done = pool, base, 0

            def wait(self):
                self.done += 1
                self.pool.wait_ge(ln_steps, self.base + self.done)

            def __call__(self, out, a, b, op):
                nc.gpsimd.tensor_tensor(out, a, b, op).then_inc(ln_steps, 1)
                self.wait()

        def layer_norm(pool, step, src, sums_base, dst, after_mean=None, stored=None):
            pool.wait_ge(ln_sums, sums_base + 1)
            nc.gpsimd.tensor_tensor(ln_mean[:, :], ln_sum[:, :], neg_inv_d[:, :], ALU.mult).then_inc(ln_steps, 1)
            if after_mean:
                after_mean()
            step.wait()
            step(ln_c[:, :, :], src[:, :, :], spread(ln_mean[:, :]), ALU.add)
            pool.wait_ge(ln_sums, sums_base + 2)
            step(ln_var[:, :], ln_sum[:, :], inv_d[:, :], ALU.mult)
            step(ln_var[:, :], ln_var[:, :], eps_tile[:, :], ALU.add)
            step(ln_rstd[:, :], ln_var[:, :], minus_half[:, :], ALU.pow)
            if stored is not None:
                pool.wait_ge(ln_stored, stored)
            step(dst[:, :, :], ln_c[:, :, :], spread(ln_rstd[:, :]), ALU.mult)

        def edges_may_survive(eng):
            eng.wait_ge(flag_made, 1)
            return eng.value_load(flag[0:1, 0:1], min_val=0, max_val=1)

        STAGES = 9
        PROJECT, EDGES, ATTEND, COMPRESS, TURN_XN, PRUNE, NODES, GATHER, SCATTER = range(STAGES)
        SHARERS = 4
        CHUNKS = N // CH

        def meet(eng, l, stage):
            eng.drain().then_inc(gate, 1)
            eng.wait_ge(gate, (l * STAGES + (stage + 1)) * SHARERS)
            eng.sem_inc(passed, 1)


        def sp_score_rows(sp, l, k):
            with sp.Fori(0, T) as i:
                n = (l * 2 + k) * T + i
                sp.dma_start(h_rows[:, :], adj[bass.ds(i * P, P), :]).then_inc(h_loaded, 16)
                if k == 1:
                    sp.wait_ge(pruned_made, l * T + i + 1)
                    sp.dma_start(pruned[bass.ds(i * P, P), :], logits[:, :]).then_inc(pruned_stored, 16)
                sp.wait_ge(row_folded, n + 1)
                sp.sem_inc(passed, 1)

        def message_sp(sp):
            for dst, src in ((w_qv_sb[:, :], w_qv), (w_q_sb[:, :], w_q), (theta2[half(0), :], theta),
                             (theta2[half(1), :], theta), (b_q_sb[:, :], b_q),
                             (b_v_sb[:, :], b_v.partition_broadcast(P))):
                sp.dma_start(dst, src).then_inc(weights_loaded, 16)
            sp.wait_ge(weights_loaded, 16 * 6)
            with sp.Fori(0, ROUNDS) as l:
                meet(sp, l, PROJECT)
                meet(sp, l, EDGES)
                with sp.Fori(0, T // RING) as it:
                    load_rows(sp, adj, l * 2 + 1, it)
                meet(sp, l, ATTEND)
                sp_score_rows(sp, l, 0)
                meet(sp, l, COMPRESS)
                meet(sp, l, TURN_XN)
                meet(sp, l, PRUNE)
                sp_score_rows(sp, l, 1)
                sp.wait_ge(pruned_stored, (l + 1) * T * 16)
                sp.sem_inc(passed, 1)
                meet(sp, l, NODES)
                meet(sp, l, GATHER)
                with sp.Fori(0, T // RING) as it:
                    load_rows(sp, pruned, l * 2 + 2, it)
                meet(sp, l, SCATTER)
                with sp.Fori(0, GROUPS // 2) as it:
                    load_tiles(sp, pruned, l + 1, it, range(2 * CUTS))
            meet(sp, ROUNDS, PROJECT)

        def pe_score_rows(pe, l, k):
            moving = edge_t if k == 0 else xt_all
            with pe.Fori(0, T) as i:
                n = (l * 2 + k) * T + i
                pe.wait_ge(row_staged, n + 1)
                for c in range(CHUNKS):
                    if c >= 4:
                        pe.wait_ge(chunk_masked, n * CHUNKS + (c - 3))
                    pe.matmul(bank[c % 4][:, :], xt_tile[:, :], moving[:, CH * c:CH * c + CH],
                              start=True, stop=True).then_inc(chunk_scored, 1)
                if k == 0:
                    pe.wait_ge(recip_ready, n + 1)
                    for j in range(T):
                        mm = pe.matmul(bank[4][:, j:j + 1], logits[:, P * j:P * j + P], recip[:, :],
                                       start=True, stop=True)
                else:
                    pe.wait_ge(pruned_made, l * T + i + 1)
                    for b in range(BLOCKS):
                        for a in range(QUADS):
                            c0 = QCOLS * a + 32 * b
                            mm = pe.matmul(bank[4][32 * a:32 * a + 32, b:b + 1], logits[:, c0:c0 + 32],
                                           ones[:, 0:1], start=True, stop=True)
                mm.then_inc(row_folded, 1)

        def act_score_rows(act, l, k):
            with act.Fori(0, T) as i:
                n = (l * 2 + k) * T + i
                act.wait_ge(max_ready, n + 1)
                nc.scalar.activation(logits[:, :], logits[:, :], ACT.Exp, bias=neg_max[:, :],
                                     accum_out=part_sum[:, :]).then_inc(exp_ready, 1)

        def dve_score_rows(dve, l, k):
            with dve.Fori(0, T) as i:
                n = (l * 2 + k) * T + i
                nc.vector.tensor_copy(xt_tile[:, :], xt_all[:, bass.ds(i * P, P)]).then_inc(row_staged, 1)
                dve.wait_ge(h_loaded, (n + 1) * 16)
                for c in range(CHUNKS):
                    cs = slice(CH * c, CH * c + CH)
                    dve.wait_ge(chunk_scored, n * CHUNKS + (c + 1))
                    nc.vector.scalar_tensor_tensor(logits[:, cs], bank[c % 4][:, :], SCALE if k == 0 else 1.0,
                                                   h_rows[:, cs], ALU.mult, ALU.mult).then_inc(chunk_masked, 1)
                dve.wait_ge(chunk_masked, (n + 1) * CHUNKS)
                nc.vector.tensor_reduce(neg_max[:, :], logits[:, :], X, ALU.max, negate=True).then_inc(max_ready, 1)
                dve.wait_ge(exp_ready, n + 1)
                nc.vector.reciprocal(recip[:, :], part_sum[:, :]).then_inc(recip_ready, 1)
                if k == 0:
                    dve.wait_ge(row_folded, n + 1)
                    nc.vector.tensor_tensor(att[:, :], att[:, :], bank[4][:, 0:T], ALU.add).then_inc(edges_kept, 1)
                else:
                    dve.wait_ge(recip_ready, n + 1)
                    nc.vector.tensor_scalar(logits[:, :], logits[:, :], recip[:, :], threshold[:, :],
                                            ALU.mult, ALU.is_ge).then_inc(edges_kept, 1)
                    nc.vector.tensor_copy(mask_tile[:, :], comp_mask[:, bass.ds(i, 1)]).then_inc(mask_staged, 1)
                    dve.wait_ge(edges_kept, n + 1)
                    dve.wait_ge(mask_staged, l * T + i + 1)
                    nc.vector.scalar_tensor_tensor(logits[:, :], logits[:, :], mask_tile[:, :], h_rows[:, :],
                                                   ALU.mult, ALU.mult,
                                                   accum_out=conn_tile[:, :]).then_inc(pruned_made, 1)
                    dve.wait_ge(pruned_made, l * T + i + 1)
                    nc.vector.tensor_copy(conn[:, bass.ds(i, 1)], conn_tile[:, :])
                    dve.wait_ge(row_folded, n + 1)
                    nc.vector.tensor_tensor(edge_deg[:, :], edge_deg[:, :], bank[4][:, 0:BLOCKS],
                                            ALU.add).then_inc(row_added, 1)
                    dve.wait_ge(pruned_stored, (l * T + i + 1) * 16)
                    dve.wait_ge(row_added, l * T + i + 1)

        def node_chain(engine, l, stage):
            count, before = [0], 0 if stage == COMPRESS else COMPRESS_STEPS

            def step(who, make):
                if who is engine:
                    if count[0]:
                        engine.wait_ge(node_steps, l * (COMPRESS_STEPS + NODES_STEPS) + (before + count[0]))
                    make().then_inc(node_steps, 1)
                count[0] += 1

            v, a, p = nc.vector, nc.scalar, nc.tensor

            def tiles_of(ap):
                return ap.unsqueeze(2).to_broadcast([P, T, D])

            def sum_squares_of(src, dst):
                step(v, lambda: v.tensor_tensor(tmp, src, src, ALU.mult))
                step(v, lambda: v.tensor_reduce(dst, tmp, X, ALU.add))
                step(v, lambda: v.tensor_scalar(dst, dst, 1e-16, None, ALU.max))

            def softmax_mask(z, e, mask):
                step(v, lambda: v.tensor_reduce(part[:, :], z, X, ALU.max))
                step(v, lambda: v.tensor_scalar(diagonal[:, :], ident[:, :], part[:, :], None, ALU.mult))
                step(p, lambda: p.matmul(bank[0][:, 0:P], ones[:, :], diagonal[:, :], start=True, stop=True))
                step(v, lambda: v.tensor_reduce(neg_max[:, :], bank[0][:, 0:P], X, ALU.max, negate=True))
                step(a, lambda: a.activation(e, z, ACT.Exp, bias=neg_max[:, :], accum_out=part_sum[:, :]))
                step(p, lambda: p.matmul(bank[1][:, 0:1], ones[:, :], part_sum[:, :], start=True, stop=True))
                step(v, lambda: v.reciprocal(recip[:, :], bank[1][:, 0:1]))
                step(v, lambda: v.tensor_scalar(mask, e, recip[:, :], threshold[:, :], ALU.mult, ALU.is_ge))

            if stage == COMPRESS:
                sum_squares_of(xw_all[:, :, :], node_a[:, :])
                step(a, lambda: a.activation(node_b[:, :], node_a[:, :], ACT.Sqrt))
                step(v, lambda: v.tensor_scalar(att[:, :], att[:, :], 0.5 / N, None, ALU.mult))
                step(v, lambda: v.scalar_tensor_tensor(node_a[:, :], node_b[:, :], 0.5, att[:, :],
                                                       ALU.mult, ALU.add))
                softmax_mask(node_a[:, :], node_b[:, :], comp_mask[:, :])
                step(v, lambda: v.tensor_tensor(x_all[:, :, :], x_all[:, :, :], tiles_of(comp_mask[:, :]), ALU.mult))
                sum_squares_of(x_all[:, :, :], node_a[:, :])
                step(a, lambda: a.activation(feat_mag[:, :], node_a[:, :], ACT.Sqrt))
                step(v, lambda: v.tensor_scalar(node_a[:, :], feat_mag[:, :], 1e-8, None, ALU.max))
                step(v, lambda: v.reciprocal(node_b[:, :], node_a[:, :]))
                step(v, lambda: v.tensor_tensor(rows_in[:, :, :], x_all[:, :, :], tiles_of(node_b[:, :]), ALU.mult))
            else:
                step(v, lambda: v.tensor_tensor(node_a[:, :], conn[:, :], feat_mag[:, :], ALU.mult))
                softmax_mask(node_a[:, :], node_b[:, :], node_c[:, :])
                step(v, lambda: v.tensor_scalar(node_a[:, :], conn[:, :], 0.0, None, ALU.is_gt))
                step(v, lambda: v.tensor_tensor(node_c[:, :], node_c[:, :], node_a[:, :], ALU.mult))
                step(v, lambda: v.tensor_tensor(node_c[:, :], node_c[:, :], comp_mask[:, :], ALU.mult))
                step(v, lambda: v.tensor_scalar(node_a[:, :], conn[:, :], DEG_EPS, None, ALU.max))
                step(a, lambda: a.activation(node_b[:, :], node_a[:, :], ACT.Sqrt))
                step(v, lambda: v.reciprocal(dv[:, :], node_b[:, :]))
                step(v, lambda: v.tensor_tensor(node_c[:, :], node_c[:, :], dv[:, :], ALU.mult))
                step(v, lambda: v.tensor_tensor(rows_in[:, :, :], xw_all[:, :, :], tiles_of(node_c[:, :]), ALU.mult))
                step(v, lambda: v.tensor_scalar(edge_deg[:, :], edge_deg[:, :], DEG_EPS, None, ALU.max))
                step(v, lambda: v.reciprocal(node_a[:, :], edge_deg[:, :]))
            assert count[0] == (COMPRESS_STEPS if stage == COMPRESS else NODES_STEPS)

        COMPRESS_STEPS, NODES_STEPS = 22, 19

        def pe_turn_x(pe, l, k):
            with pe.Fori(0, T) as i:
                n = (l * 2 + k) * T + i
                pe.wait_ge(x_staged, n + 1)
                pe.transpose(bank[0][:, 0:P], x_pad[:, :], ident[:, :]).then_inc(x_turned, 1)
                if k == 0:
                    pe.wait_ge(xt_ready, n + 1)
                    pe.matmul(bank[1][:, 0:2 * D], xt_tile[:, :], w_qv_sb[:, :], start=True, stop=True)
                    pe.matmul(bank[2][0:D, 0:P], w_q_sb[:, :], xt_tile[:, :],
                              start=True, stop=True).then_inc(projected, 1)

        def message_pe(pe):
            with pe.Fori(0, ROUNDS) as l:
                meet(pe, l, PROJECT)
                pe_turn_x(pe, l, 0)
                meet(pe, l, EDGES)
                clear_sums(pe)
                with pe.Fori(0, T // RING) as it:
                    multiply_rows(pe, l * 2 + 1, it)
                meet(pe, l, ATTEND)
                pe_score_rows(pe, l, 0)
                meet(pe, l, COMPRESS)
                node_chain(pe, l, COMPRESS)
                meet(pe, l, TURN_XN)
                pe_turn_x(pe, l, 1)
                meet(pe, l, PRUNE)
                pe_score_rows(pe, l, 1)
                meet(pe, l, NODES)
                node_chain(pe, l, NODES)
                meet(pe, l, GATHER)
                clear_sums(pe)
                with pe.Fori(0, T // RING) as it:
                    multiply_rows(pe, l * 2 + 2, it)
                turn_cols(pe, l + 1)
                meet(pe, l, SCATTER)
                with pe.Fori(0, GROUPS // 2) as it:
                    multiply_tiles(pe, l + 1, it, theta2)
            meet(pe, ROUNDS, PROJECT)

        def act_turn_x(act, l, k):
            with act.Fori(0, T) as i:
                n = (l * 2 + k) * T + i
                act.wait_ge(x_turned, n + 1)
                if k == 0:
                    act.copy(xt_tile[:, :], bank[0][0:D, 0:P]).then_inc(xt_ready, 1)
                    act.wait_ge(projected, l * T + i + 1)
                    nc.scalar.activation(xt_all[:, bass.ds(i * P, P)], bank[2][0:D, 0:P], ACT.Identity,
                                         bias=b_q_sb[:, :]).then_inc(q_kept, 1)
                else:
                    act.copy(xt_all[:, bass.ds(i * P, P)], bank[0][0:D, 0:P]).then_inc(xt_ready, 1)

        def message_act(act):
            with act.Fori(0, ROUNDS) as l:
                meet(act, l, PROJECT)
                act_turn_x(act, l, 0)
                meet(act, l, EDGES)
                with act.Fori(0, T // RING) as it:
                    stage_rows(act, l * 2 + 1, it)
                act.wait_ge(rows_used, (l * 2 + 2) * T)
                for b in range(BANKS):
                    for h in range(2):
                        c0 = HALF * h + CH * b
                        act.copy(edge_t[:, c0:c0 + CH], bank[b][half(h), :])
                meet(act, l, ATTEND)
                act_score_rows(act, l, 0)
                meet(act, l, COMPRESS)
                node_chain(act, l, COMPRESS)
                meet(act, l, TURN_XN)
                act_turn_x(act, l, 1)
                meet(act, l, PRUNE)
                act_score_rows(act, l, 1)
                meet(act, l, NODES)
                node_chain(act, l, NODES)
                meet(act, l, GATHER)
                with act.Fori(0, T // RING) as it:
                    stage_rows(act, l * 2 + 2, it)
                act.wait_ge(rows_used, (l * 2 + 3) * T)
                for b in range(BANKS):
                    copy_cols(act, b)
                meet(act, l, SCATTER)
                with act.Fori(0, GROUPS // 2) as it:
                    for k in range(2):
                        copy_sums(act, l + 1, it, k)
            meet(act, ROUNDS, PROJECT)
            act.wait_ge(msg_added, 1)
            with act.Fori(0, GROUPS) as g:
                p0 = g * STEPS1 + GROUPS * STEPS0
                for t in range(TPG):
                    last = nc.scalar.activation(ln_h[:, t, :], x_all[:, bass.ds(g * TPG + t, 1), :].squeeze(1),
                                                ACT.Copy, accum_out=ln_sum[:, t:t + 1])
                last.then_inc(ln_sums, 1)
                act.wait_ge(ln_steps, p0 + 2)
                sum_squares(act)
                act.wait_ge(ln_steps, p0 + STEPS1)
                store_group(act, g)
            act.wait_ge(ln_stored, 16 * (2 * GROUPS + 1))

        def dve_turn_x(dve, l, k):
            src = x_all if k == 0 else rows_in
            with dve.Fori(0, T) as i:
                n = (l * 2 + k) * T + i
                nc.vector.tensor_copy(x_pad[:, 0:D], src[:, bass.ds(i, 1), :].squeeze(1)).then_inc(x_staged, 1)
                if k == 0:
                    m = l * T + i + 1
                    dve.wait_ge(projected, m)
                    nc.vector.tensor_copy(xw_all[:, bass.ds(i, 1), :].squeeze(1), bank[1][:, 0:D])
                    nc.vector.tensor_tensor(rows_in[:, bass.ds(i, 1), :].squeeze(1), bank[1][:, D:2 * D],
                                            b_v_sb[:, :], ALU.add).then_inc(row_kept, 1)
                    dve.wait_ge(q_kept, m)
                    dve.wait_ge(row_kept, m)
                else:
                    dve.wait_ge(xt_ready, n + 1)

        def message_dve(dve):
            dve.wait_ge(ln_stored, 16 * (GROUPS + 1))
            nc.vector.tensor_copy(x_all[:, :, :], x1_all[:, :, :])
            nc.vector.memset(ones[:, :], 1.0)
            nc.vector.memset(x_pad[:, :], 0.0)
            for r in range(ROUNDS):
                nc.vector.memset(thresholds[:, r:r + 1], THETA[r])
            with dve.Fori(0, ROUNDS) as l:
                meet(dve, l, PROJECT)
                nc.vector.tensor_copy(threshold[:, :], thresholds[:, bass.ds(l, 1)])
                nc.vector.memset(att[:, :], 0.0)
                nc.vector.memset(edge_deg[:, :], 0.0)
                dve_turn_x(dve, l, 0)
                meet(dve, l, EDGES)
                meet(dve, l, ATTEND)
                dve_score_rows(dve, l, 0)
                meet(dve, l, COMPRESS)
                node_chain(dve, l, COMPRESS)
                meet(dve, l, TURN_XN)
                dve_turn_x(dve, l, 1)
                meet(dve, l, PRUNE)
                dve_score_rows(dve, l, 1)
                meet(dve, l, NODES)
                node_chain(dve, l, NODES)
                meet(dve, l, GATHER)
                for b in range(BANKS):
                    dve.wait_ge(cols_turned, (l + 1) * BANKS + (b + 1))
                    nc.vector.tensor_tensor(cols[:, 8 * b:8 * b + 8, :],
                                            bank[b][:, :].rearrange("p (t d) -> p t d", d=D),
                                            node_a[:, 8 * b:8 * b + 8].unsqueeze(2).to_broadcast([P, 8, D]), ALU.mult)
                meet(dve, l, SCATTER)
                with dve.Fori(0, GROUPS // 2) as it:
                    for k in range(2):
                        turn_tiles(dve, l + 1, it, range(k * CUTS, k * CUTS + CUTS))
                        g = it * 2 + k
                        dve.wait_ge(nat_ready, g + ((l + 1) * GROUPS + 1))
                        nc.vector.tensor_tensor(ln_c[:, :, :], nat_bank[:, 0:TPG * D].rearrange("p (t d) -> p t d", d=D),
                                                dv[:, bass.ds(g * TPG, TPG)].unsqueeze(2).to_broadcast([P, TPG, D]),
                                                ALU.mult).then_inc(nat_read, 1)
                        dve.wait_ge(nat_read, g + ((l + 1) * GROUPS + 2))
                        nc.vector.tensor_scalar(x_all[:, bass.ds(g * TPG, TPG), :], ln_c[:, :, :], 0.0, None,
                                                ALU.max).then_inc(msg_kept, 1)
                        dve.wait_ge(msg_kept, g + (l * GROUPS + 1))
            meet(dve, ROUNDS, PROJECT)
            nc.vector.tensor_tensor(x_all[:, :, :], x_all[:, :, :], x1_all[:, :, :], ALU.add).then_inc(msg_added, 1)

        def message_pool(pool):
            pool.wait_ge(gate, (ROUNDS * STAGES + 1) * SHARERS)
            with pool.Fori(0, GROUPS) as g:
                step = Steps(pool, g * STEPS1 + GROUPS * STEPS0)
                layer_norm(pool, step, ln_h, g * SUMS1 + GROUPS * SUMS0, ln_out,
                           stored=(g + (GROUPS + 1)) * 16)

        @block.sync
        def _(sp):
            sp.dma_start(xt_all, x_t).then_inc(const_loaded, 16)
            sp.dma_start(w_ui_sb[:, :], w_ui).then_inc(const_loaded, 16)
            sp.dma_start(x_all[:, :, :], x.rearrange("(t p) d -> p t d", p=P)).then_inc(const_loaded, 16)
            sp.dma_start(diag_sb[:, :], diag).then_inc(const_loaded, 16)
            sp.dma_start(par_sb[:, :], par.partition_broadcast(P)).then_inc(const_loaded, 16)
            load_rows(sp, adj, L0, 0, first=True)
            with sp.Fori(1, T // RING) as it:
                load_rows(sp, adj, L0, it)
            load_tiles(sp, adj, L0, 0, range(RING), first=True)
            load_tiles(sp, adj, L0, 0, range(RING, 2 * CUTS))
            with sp.Fori(1, GROUPS // 2) as it:
                load_tiles(sp, adj, L0, it, range(2 * CUTS))
            with sp.If(edges_may_survive(sp) > 0):
                message_sp(sp)

        @block.gpsimd
        def _(pool):
            nc.gpsimd.memset(ident[:, :], 0.0).then_inc(ident_clear, 1)
            nc.gpsimd.memset(stack[:, :], 0.0).then_inc(ident_clear, 1)
            for tile, value in ((minus_half, -0.5), (inv_d, 1.0 / D), (neg_inv_d, -1.0 / D), (eps_tile, LN_EPS)):
                nc.gpsimd.memset(tile[:, :], value).then_inc(ident_clear, 1)
            pool.wait_ge(ident_clear, 6)
            nc.gpsimd.affine_select(out=ident[:, :], in_=ident[:, :], compare_op=ALU.not_equal, fill=1.0,
                                    base=0, pattern=[[-1, P]], channel_multiplier=1).then_inc(const_made, 1)
            for h in range(2):
                pool.wait_ge(const_made, 1 + h)
                nc.gpsimd.affine_select(out=stack[:, :], in_=stack[:, :], compare_op=ALU.not_equal, fill=1.0,
                                        base=-D * h, pattern=[[-1, D]],
                                        channel_multiplier=1).then_inc(const_made, 1)
            pool.wait_ge(max_found, 1)
            nc.gpsimd.partition_all_reduce(all_max[:, :], part_max[:, :], P, bass.bass_isa.ReduceOp.max).then_inc(max_found, 1)
            pool.wait_ge(max_found, 2)
            nc.gpsimd.tensor_scalar(flag[:, :], all_max[:, :], LIMIT, None, ALU.is_ge).then_inc(flag_made, 1)

            pool.sem_inc(ln_stored, 16)
            pool.wait_ge(small_loaded, 16 * 2)
            with pool.Fori(0, GROUPS) as g:
                s0 = g * SUMS0
                step = Steps(pool, g * STEPS0)
                tiles = bass.ds(g * TPG, TPG)
                layer_norm(pool, step, ln_h, s0, ln_y,
                           after_mean=lambda: nc.gpsimd.tensor_copy(ln_x[:, :, :], x_all[:, tiles, :]))
                step(ln_y[:, :, :], ln_y[:, :, :], over_tiles(gamma_sb[:, :]), ALU.mult)
                step(ln_y[:, :, :], ln_y[:, :, :], over_tiles(beta_sb[:, :]), ALU.add)
                step(ln_y[:, :, :], ln_y[:, :, :], ln_x[:, :, :], ALU.add)
                step(ln_h[:, :, :], ln_y[:, :, :], ln_x[:, :, :], ALU.add)
                layer_norm(pool, step, ln_h, s0 + 2, ln_y)
                layer_norm(pool, step, ln_y, s0 + 4, ln_out, stored=(g + 1) * 16,
                           after_mean=lambda: nc.gpsimd.tensor_copy(x1_all[:, tiles, :], ln_y[:, :, :]))
            with pool.If(edges_may_survive(pool) > 0):
                message_pool(pool)

        @block.scalar
        def _(act):
            act.dma_start(gamma_sb[:, :], gamma.partition_broadcast(P)).then_inc(small_loaded, 16)
            act.dma_start(beta_sb[:, :], beta.partition_broadcast(P)).then_inc(small_loaded, 16)
            act.wait_ge(e_made, BANKS)
            stage_rows(act, L0, 0, first=True)
            with act.Fori(1, T // RING) as it:
                stage_rows(act, L0, it)
            act.wait_ge(rows_used, T)
            for b in range(BANKS):
                copy_cols(act, b)
            for b in range(BANKS):
                act.wait_ge(cols_turned, b + 1)
                act.copy(cols[:, 8 * b:8 * b + 8, :], bank[b][:, :]).then_inc(cols_ready, 1)
            with act.Fori(0, GROUPS // 2) as it:
                for k in range(2):
                    g = it * 2 + k
                    copy_sums(act, L0, it, k)
                    s0, p0 = g * SUMS0, g * STEPS0
                    act.wait_ge(nat_ready, g + 1)
                    for t in range(TPG):
                        last = nc.scalar.activation(ln_h[:, t, :], nat_bank[:, D * t:D * t + D], ACT.Copy,
                                                    accum_out=ln_sum[:, t:t + 1])
                    last.then_inc(ln_sums, 1)
                    act.wait_ge(ln_sums, s0 + 1)
                    act.sem_inc(nat_read, 1)
                    for first, src in ((2, None), (LN_STEPS + 4, ln_h), (LN_STEPS + 6, None),
                                       (2 * LN_STEPS + 4, ln_y), (2 * LN_STEPS + 6, None)):
                        act.wait_ge(ln_steps, p0 + first)
                        sum_squares(act) if src is None else sum_features(act, src)
                    act.wait_ge(ln_steps, p0 + STEPS0)
                    store_group(act, g)
            act.wait_ge(ln_stored, 16 * (GROUPS + 1))
            with act.If(edges_may_survive(act) > 0):
                message_act(act)

        @block.vector
        def _(dve):
            nc.vector.memset(zeros[:, :], 0.0).then_inc(zeros_made, 1)
            dve.wait_ge(const_loaded, 16 * 5)
            nc.vector.tensor_tensor(pp[:, :], par_sb[:, 0:4:2], par_sb[:, 1:4:2], ALU.mult).then_inc(pp_made, 1)
            dve.wait_ge(pp_made, 1)
            for k, (a, b) in enumerate(((0, USER_TILES), (USER_TILES, T))):
                nc.vector.tensor_scalar(diag_sb[:, a:b], diag_sb[:, a:b], pp[:, k:k + 1], None,
                                        ALU.mult).then_inc(pp_made, 1)
            dve.wait_ge(pp_made, 3)
            for b in range(BANKS):
                dve.wait_ge(xw_done, b + 1)
                t8 = slice(8 * b, 8 * b + 8)
                nc.vector.tensor_tensor(rows_in[:, t8, :], bank[b][:, :].rearrange("p (t d) -> p t d", d=D),
                                        diag_sb[:, t8].unsqueeze(2).to_broadcast([P, 8, D]),
                                        ALU.mult).then_inc(e_scaled, 1)
                dve.wait_ge(e_scaled, b + 1)
                nc.vector.tensor_tensor(rows_in[:, t8, :], rows_in[:, t8, :], x_all[:, t8, :],
                                        ALU.add).then_inc(e_made, 1)
            with dve.Fori(0, T // RING) as it:
                for s in range(RING):
                    dve.wait_ge(rows_loaded[s], (it + 1) * 16)
                    nc.vector.tensor_reduce(row_max[:, bass.ds(it * RING + s, 1)], ring[s][:, :], X, ALU.max,
                                            apply_absolute_value=True).then_inc(rows_scanned, 1)
            dve.wait_ge(rows_scanned, T)
            nc.vector.tensor_reduce(part_max[:, :], row_max[:, :], X, ALU.max).then_inc(max_found, 1)
            turn_tiles(dve, L0, 0, range(2), first=True)
            turn_tiles(dve, L0, 0, range(2, 2 * CUTS))
            with dve.Fori(1, GROUPS // 2) as it:
                turn_tiles(dve, L0, it, range(2 * CUTS))
            with dve.If(edges_may_survive(dve) > 0):
                message_dve(dve)

        @block.tensor
        def _(pe):
            pe.sem_inc(nat_read, 1)
            pe.wait_ge(const_loaded, 16 * 5)
            pe.wait_ge(const_made, 3)
            pe.wait_ge(zeros_made, 1)
            for t in range(T):
                k = 0 if t < USER_TILES else 1
                mm = pe.matmul(bank[t // 8][:, D * (t % 8):D * (t % 8) + D], xt_all[:, P * t:P * t + P],
                               w_ui_sb[:, D * k:D * k + D], start=True, stop=True)
                if t % 8 == 7:
                    mm.then_inc(xw_done, 1)
            pe.wait_ge(e_made, BANKS)
            clear_sums(pe)
            with pe.Fori(0, T // RING) as it:
                multiply_rows(pe, L0, it)
            turn_cols(pe, L0)
            pe.wait_ge(cols_ready, BANKS)
            with pe.Fori(0, GROUPS // 2) as it:
                multiply_tiles(pe, L0, it, stack)
            with pe.If(edges_may_survive(pe) > 0):
                message_pe(pe)


_INS = ("x", "x_t", "adj", "w_ui", "diag", "par", "gamma", "beta", "w_qv", "w_q", "theta", "b_q", "b_v")


def kernel(**inputs):
    import numpy as np
    import concourse.bacc as bacc
    from concourse.bass_utils import run_bass_kernel_spmd as run

    a = {k: np.asarray(v) for k, v in inputs.items()}
    laid = {
        "x": a["x"],
        "x_t": np.ascontiguousarray(a["x"].T),
        "adj": a["adj"],
        "w_ui": np.concatenate([a["L0_gnn_W_u"], a["L0_gnn_W_i"]], axis=1),
        "diag": np.ascontiguousarray(np.concatenate([a["L0_gnn_diag_u"], a["L0_gnn_diag_i"]]).reshape(-1, 128).T),
        "par": np.concatenate([a["L0_gnn_par_u"], a["L0_gnn_par_i"]]),
        "gamma": a["L0_gnn_ln_gamma"],
        "beta": a["L0_gnn_ln_beta"],
        "w_qv": np.concatenate([a["L1_gnn_W"], a["L1_gnn_Wv"]], axis=1),
        "w_q": a["L1_gnn_Wq"],
        "theta": a["L1_gnn_Theta"],
        "b_q": a["L1_gnn_bq"].reshape(-1, 1),
        "b_v": a["L1_gnn_bv"],
    }
    nc = bacc.Bacc("TRN2", target_bir_lowering=False, num_devices=1)
    arrays, args = {}, []
    for name in _INS:
        v = np.ascontiguousarray(laid[name])
        arrays[f"in_{name}"] = v
        args.append(nc.dram_tensor(f"in_{name}", v.shape, mybir.dt.from_np(v.dtype), kind="ExternalInput").ap())
    shape = a["x"].shape
    args.append(nc.dram_tensor("out_0", shape, mybir.dt.from_np(a["x"].dtype), kind="ExternalOutput").ap())
    adjacency_layers_kernel(nc, *args)
    r = run(nc, [arrays], core_ids=[0])
    return r.results[0]["out_0"]
```

```python
import math
from contextlib import ExitStack

import concourse.bass as bass
from concourse import mybir



def adjacency_layers_kernel(nc, x, adj, w_ui, diag, par, gamma, beta,
                            w_qv, w_q, theta, b_q, b_v, out):
    f32 = mybir.dt.float32
    i32 = mybir.dt.int32
    ALU = mybir.AluOpType
    ACT = mybir.ActivationFunctionType
    X = mybir.AxisListType.X

    P = 128
    N, D = x.shape
    T = N // P
    USER_TILES = 2048 // P
    CH = 512
    BANKS = N // (2 * CH)
    HALF = N // 2
    RING = 4
    SPARE = 2
    QUADS = 4
    QCOLS = N // QUADS
    BLOCKS = QCOLS // 32
    CUTS = 4
    BPT = BLOCKS // CUTS
    GROUP = 512
    GROUPS = N // GROUP
    TPG = GROUP // P
    RSUB = GROUP // 32
    KEPT = GROUPS - 1
    FLIPS = T // 4
    STEPS = RING * FLIPS
    EARLY = RING * CUTS
    BURST = -(-STEPS // (EARLY - 1))
    LN_EPS = 1e-5
    DEG_EPS = 1e-6
    SCALE = float(D) ** -0.5
    ROUNDS = 2
    THETA = [0.000244 + (1.0 - math.exp(-0.1 * it)) * (0.0003 - 0.000244) for it in range(ROUNDS)]
    LIMIT = 0.5 * math.log(N * THETA[0]) - 0.01

    pruned = nc.dram_tensor("pruned_adjacency", [N, N], f32, kind="Internal").ap()

    ctx = ExitStack()
    with ctx:
        def sb(name, shape, dt=f32):
            return ctx.enter_context(nc.sbuf_tensor(name, shape, dt))

        def sem(name):
            return ctx.enter_context(nc.semaphore(name))

        ring = [sb(f"ring{s}", [P, N]) for s in range(RING + SPARE)]
        turned = [sb(f"turned{s}", [P, N]) for s in range(2)]
        x_all = sb("x_all", [P, T, D])
        rows_in = sb("rows_in", [P, T, D])
        cols = sb("cols", [P, BLOCKS, D])
        sums = [sb(f"sums{s}", [P, GROUP]) for s in range(2)]
        flipped = [sb(f"flipped{s}", [P, CH]) for s in range(BURST)]
        staged = [flipped[1][:, TPG * D + D * s:TPG * D + D * s + D] for s in range(RING)]
        ident = sb("ident", [P, P])
        stack = sb("stack", [P, D])
        zeros = sums[0]
        w_ui_sb = sb("w_ui_sb", [P, 2 * D])
        diag_sb = sb("diag_sb", [P, T])
        par_sb = sb("par_sb", [P, 4])
        pp = sb("pp", [P, 2])
        gamma_sb = sb("gamma_sb", [P, D])
        beta_sb = sb("beta_sb", [P, D])
        row_max = sb("row_max", [P, T])
        part_max = sb("part_max", [P, 1])
        all_max = sb("all_max", [P, 1])
        flag = sb("flag", [P, 1], i32)
        ln_h = sb("ln_h", [P, TPG, D])
        ln_c = sb("ln_c", [P, TPG, D])
        ln_y = sb("ln_y", [P, TPG, D])
        ln_sum = sb("ln_sum", [P, TPG])
        ln_mean = sb("ln_mean", [P, TPG])
        ln_var = sb("ln_var", [P, TPG])
        ln_rstd = sb("ln_rstd", [P, TPG])
        ln_out = sb("ln_out", [P, TPG, D])
        ln_x = sb("ln_x", [P, TPG, D])
        minus_half = sb("minus_half", [P, TPG])
        inv_d = sb("inv_d", [P, TPG])
        neg_inv_d = sb("neg_inv_d", [P, TPG])
        eps_tile = sb("eps_tile", [P, TPG])
        end_stats = sb("end_stats", [P, TPG, 6])
        end_mv = sb("end_mv", [P, TPG, 2])
        end_var = sb("end_var", [P, TPG])
        end_rstd = sb("end_rstd", [P, TPG])
        end_y, end_add = [flipped[i][:, 0:TPG * D].rearrange("p (t d) -> p t d", d=D)
                          for i in range(2)]

        cols_t = turned[1][0:D, :]
        cols_nat = rows_in

        xt_pairs = turned[0][:, 0:T // 2 * P]

        carved = [T * D]

        def carve(width, parts=P):
            carved[0] += width
            return ring[RING][0:parts, carved[0] - width:carved[0]]

        x_cur = ring[RING][:, 0:T * D].rearrange("p (t d) -> p t d", d=D)
        w_qv_sb = carve(2 * D, D)
        w_q_sb = carve(D, D)
        theta2 = carve(D)
        b_q_sb = carve(1, D)
        b_v_sb = carve(D)
        thresholds = carve(ROUNDS)
        threshold = carve(1)
        x_pad = carve(P)
        xt_tile = carve(P, D)
        ones = carve(P)
        diagonal = carve(P)
        node_a, node_b, node_c = carve(T), carve(T), carve(T)
        att = carve(T)
        comp_mask = carve(T)
        feat_mag = carve(T)
        conn = carve(T)
        edge_deg = carve(BLOCKS)
        dv = carve(T)
        part, neg_max, part_sum, recip, mask_tile, conn_tile = (carve(1) for _ in range(6))

        xt_all = turned[0][0:D, :]
        edge_t = turned[1][0:D, :]
        h_rows, logits = ring[0], ring[1]
        tmp = ring[2][:, 0:T * D].rearrange("p (t d) -> p t d", d=D)
        xw_all = cols

        bank = [ctx.enter_context(nc.psum_tensor(f"bank{b}", [P, CH], f32)) for b in range(8)]
        sum_bank = [bank[5], bank[6]]
        nat_bank = [bank[0], bank[7]]
        kept_bank = bank[4]
        flip_bank = [bank[1 + i] for i in range(BURST)]

        const_loaded = sem("const_loaded")
        x_loaded = sem("x_loaded")
        const_made = sem("const_made")
        ident_clear = sem("ident_clear")
        pp_made = sem("pp_made")
        pairs_turned = sem("pairs_turned")
        pairs_copied = sem("pairs_copied")
        xw_done = sem("xw_done")
        e_scaled = sem("e_scaled")
        e_made = sem("e_made")
        rows_loaded = [sem(f"rows_loaded{s}") for s in range(RING)]
        tile_staged = sem("tile_staged")
        rows_used = sem("rows_used")
        rows_scanned = sem("rows_scanned")
        cols_copied = sem("cols_copied")
        cols_turned = sem("cols_turned")
        tiles_loaded = [sem(f"tiles_loaded{s}") for s in range(RING)]
        halves_turned = sem("halves_turned")
        end_loaded = sem("end_loaded")
        spare_loaded = [sem(f"spare_loaded{s}") for s in range(SPARE)]
        cols_made = sem("cols_made")
        cols_nat_ready = sem("cols_nat_ready")
        blocks_flipped = sem("blocks_flipped")
        blocks_copied = sem("blocks_copied")
        flipped_used = sem("flipped_used")
        add_made = sem("add_made")
        end_steps = sem("end_steps")
        end_stored = sem("end_stored")
        tiles_used = sem("tiles_used")
        sums_copied = sem("sums_copied")
        nat_ready = sem("nat_ready")
        nat_read = sem("nat_read")
        ln_sums = sem("ln_sums")
        ln_steps = sem("ln_steps")
        ln_stored = sem("ln_stored")
        max_found = sem("max_found")
        flag_made = sem("flag_made")
        weights_loaded = sem("weights_loaded")
        gate = sem("gate")
        passed = sem("passed")
        x_staged = sem("x_staged")
        x_turned = sem("x_turned")
        xt_ready = sem("xt_ready")
        projected = sem("projected")
        q_kept = sem("q_kept")
        h_loaded = sem("h_loaded")
        row_staged = sem("row_staged")
        chunk_scored = sem("chunk_scored")
        chunk_masked = sem("chunk_masked")
        max_ready = sem("max_ready")
        exp_ready = sem("exp_ready")
        recip_ready = sem("recip_ready")
        edges_kept = sem("edges_kept")
        pruned_made = sem("pruned_made")
        pruned_stored = sem("pruned_stored")
        row_folded = sem("row_folded")
        node_steps = sem("node_steps")
        mask_staged = sem("mask_staged")
        row_kept = sem("row_kept")
        row_added = sem("row_added")
        msg_kept = sem("msg_kept")
        msg_added = sem("msg_added")
        small_loaded = sem("small_loaded")

        block = ctx.enter_context(nc.Block())

        def half(h):
            return slice(D * h, D * h + D)

        def turned_block(t, b):
            return turned[t][:, CH * b:CH * b + CH]

        def perm(ap, b):
            return ap.rearrange("p (a b c) -> p b a c", a=QUADS, b=BLOCKS)[:, b]


        def load_rows(sp, src, call, it, first=False):
            for s in range(RING):
                n = it * RING + s
                if not first:
                    sp.wait_ge(rows_used, n + (call * T + 1 - RING))
                    if call is L0:
                        sp.wait_ge(rows_scanned, n + (1 - RING))
                sp.dma_start(ring[s][:, :], src[bass.ds(n * P, P), :]).then_inc(rows_loaded[s], 16)

        def stage_rows(act, call, it, first=False):
            for s in range(RING):
                n = it * RING + s
                if not first:
                    act.wait_ge(rows_used, n + (call * T + 1 - RING))
                act.copy(staged[s][:, :], rows_in[:, bass.ds(n, 1), :]).then_inc(tile_staged, 1)

        def xw_out(b, odd):
            to = (sum_bank if b % 2 == 0 else [nat_bank[1], kept_bank])[odd]
            return to[:, 0:4 * D].rearrange("p (t d) -> p t d", d=D)

        def multiply_rows(pe, call, it, first=False):
            for s in range(RING):
                n = it * RING + s
                pe.wait_ge(rows_loaded[s], (call * (T // RING) + it + 1) * 16)
                pe.wait_ge(tile_staged, n + (call * T + 1))
                for b in range(BANKS):
                    for h in range(2):
                        mm = pe.matmul(bank[b][half(h), :], staged[s][:, :],
                                       ring[s][:, HALF * h + CH * b:HALF * h + CH * b + CH],
                                       start=(first and s == 0), stop=False, skip_group_check=True)
                mm.then_inc(rows_used, 1)

        def clear_sums(pe):
            for b in range(BANKS):
                for h in range(2):
                    mm = pe.matmul(bank[b][half(h), :], zeros[:, 0:D], zeros[:, :],
                                   start=True, stop=False, skip_group_check=True)

        def copy_cols(act, h):
            to = cols_t.rearrange("p (b a c) -> p a b c", a=QUADS, b=BLOCKS)
            for b in range(BANKS):
                first, last = (HALF * h + b * CH) // 32, (HALF * h + (b + 1) * CH) // 32
                for a in range(2 * h, 2 * h + 2):
                    lo, hi = max(first, a * BLOCKS), min(last, (a + 1) * BLOCKS)
                    if lo < hi:
                        at = bank[b][half(h), 32 * (lo - first):32 * (hi - first)]
                        copied = act.copy(to[:, a, lo - a * BLOCKS:hi - a * BLOCKS, :],
                                          at.rearrange("p (b c) -> p b c", c=32))
            copied.then_inc(cols_copied, 1)

        def turn_cols(pe, b, to):
            for j in range(8):
                c0 = P * (8 * b + j)
                mm = pe.transpose(to[:, D * j:D * j + D], cols_t[:, c0:c0 + P], ident[half(0), half(0)])
            mm.then_inc(cols_turned, 1)

        def make_cols_nat(act):
            for a in range(QUADS):
                for j in range(QUADS):
                    made = act.copy(cols_nat[32 * j:32 * j + 32, FLIPS * a:FLIPS * a + FLIPS, :],
                                    cols[32 * a:32 * a + 32, j:BLOCKS:QUADS, :])
            made.then_inc(cols_nat_ready, 1)

        def burst(n):
            return range((n - 1) * STEPS // (EARLY - 1), n * STEPS // (EARLY - 1)) if n else range(0)

        def flip_blocks(pe, n):
            for i, t in enumerate(burst(n)):
                if n >= 2 and i < len(burst(n - 1)):
                    pe.wait_ge(blocks_copied, burst(n - 1)[i] + 1)
                for j in range(4):
                    c0 = P * (4 * (t % FLIPS) + j)
                    mm = pe.transpose(flip_bank[i][:, P * j:P * j + P], ring[t // FLIPS][:, c0:c0 + P], ident[:, :])
                mm.then_inc(blocks_flipped, 1)

        def copy_flipped(act, n):
            for i, t in enumerate(burst(n)):
                act.wait_ge(blocks_flipped, t + 1)
                if burst(n)[0]:
                    act.wait_ge(flipped_used, burst(n)[0])
                act.copy(flipped[i][:, :], flip_bank[i][:, :]).then_inc(blocks_copied, 1)

        def multiply_flipped(pe, n):
            for i, t in enumerate(burst(n)):
                s = t // FLIPS
                pe.wait_ge(blocks_copied, t + 1)
                for j in range(4):
                    c = 4 * (t % FLIPS) + j
                    mm = pe.matmul(kept_bank[half(j % 2), P * s:P * s + P], cols_nat[:, c, :],
                                   flipped[i][:, P * j:P * j + P], start=(c < 2), stop=(c >= T - 2))
                mm.then_inc(flipped_used, 1)

        class Use:

            def __init__(self, groups, tiles, rounds, first_group=0):
                self.groups, self.tiles, self.rounds, self.first = groups, tiles, rounds, first_group
                self.odd = first_group % 2

        def load_tile(sp, src, slot, g, q, signals):
            dst = ring[slot][:, :].rearrange("p (R k) -> p R k", R=RSUB)
            width = BPT * 32 // len(signals)
            for h, signal in enumerate(signals):
                for a in range(QUADS):
                    c0 = QCOLS * a + q * BPT * 32 + width * h
                    piece = src[bass.ds(g * GROUP, GROUP), c0:c0 + width]
                    sp.dma_start(dst[32 * a:32 * a + 32, :, width * h:width * h + width],
                                 piece.rearrange("(R r) k -> r R k", r=32)).then_inc(signal, 16)

        def load_tiles(sp, src, use, it, units, end=False):
            for u in units:
                sp.wait_ge(halves_turned, (it * (2 * CUTS) + (use.tiles + (u + 1 - RING))) * 2)
                last = end and u == units[-1]
                load_tile(sp, src, u % RING, it * 2 + (use.first + u // CUTS), u % CUTS,
                          [end_loaded, tiles_loaded[u % RING]] if last else [tiles_loaded[u % RING]])

        def turn_half(slot, to, h):
            out = to[:, :].rearrange("p (b R r) -> p R b r", b=BPT, R=RSUB)
            tile = ring[slot][:, :].rearrange("p (R b c) -> p R b c", R=RSUB, b=BPT)
            blocks = slice(BPT // 2 * h, BPT // 2 * (h + 1))
            nc.vector.transpose(out[:, :, blocks, :], tile[:, :, blocks, :]).then_inc(halves_turned, 1)

        def turn_tile(slot, to):
            for h in range(2):
                turn_half(slot, to, h)

        def turn_tiles(dve, use, it, units, end=False):
            for u in units:
                dve.wait_ge(tiles_used, it * (2 * CUTS) + (use.tiles + (u - 1)))
                if end and u == units[-1]:
                    dve.wait_ge(end_loaded, 64)
                    turn_half(u % RING, turned[u % 2], 0)
                    dve.wait_ge(tiles_loaded[u % RING], (it * 2 + (use.rounds + (u // RING + 1))) * 64)
                    turn_half(u % RING, turned[u % 2], 1)
                else:
                    dve.wait_ge(tiles_loaded[u % RING], (it * 2 + (use.rounds + (u // RING + 1))) * 64)
                    turn_tile(u % RING, turned[u % 2])

        def multiply_tile(pe, n, k, q):
            for j in range(BPT):
                if j % (BPT // 2) == 0:
                    pe.wait_ge(halves_turned, n * 2 + (1 if j == 0 else 2))
                mm = pe.matmul(sum_bank[k][half(j % 2), :], cols[:, q * BPT + j, :],
                               turned_block(q % 2, j), start=(q == 0 and j < 2),
                               stop=(q == CUTS - 1 and j >= BPT - 2))
            mm.then_inc(tiles_used, 1)

        def close_group(pe, count, k, nat, closing):
            pe.wait_ge(sums_copied, count + 1)
            pe.wait_ge(nat_read, count + 1)
            for t in range(TPG):
                mm = pe.matmul(nat_bank[nat][:, D * t:D * t + D], sums[k][:, P * t:P * t + P],
                               closing, start=True, stop=True)
            mm.then_inc(nat_ready, 1)

        def multiply_tiles(pe, use, it, closing, closed_after):
            for u in range(2 * CUTS):
                k, q = (u // CUTS + use.odd) % 2, u % CUTS
                multiply_tile(pe, it * (2 * CUTS) + (use.tiles + u), k, q)
                if q == closed_after:
                    back = 0 if closed_after else 1
                    close_group(pe, it * 2 + (use.groups + u // CUTS - back), (k - back) % 2,
                                (u // CUTS - back) % 2, closing)

        def copy_sums(copy, k, src=None):
            copy(sums[k][:, :], (src or sum_bank[k])[:, :]).then_inc(sums_copied, 1)

        LN_STEPS = 6

        def sum_features(act, src):
            for t in range(TPG):
                last = nc.scalar.activation(ln_c[:, t, :], src[:, t, :], ACT.Copy,
                                            accum_out=ln_sum[:, t:t + 1])
            last.then_inc(ln_sums, 1)

        def sum_squares(act):
            for t in range(TPG):
                last = nc.scalar.activation(ln_y[:, t, :], ln_c[:, t, :], ACT.Square,
                                            accum_out=ln_sum[:, t:t + 1])
            last.then_inc(ln_sums, 1)

        def store_group(eng, g, src, signal):
            eng.dma_start(out.rearrange("(g t p) d -> g p t d", p=P, t=TPG)[bass.ds(g, 1)].squeeze(0),
                          src[:, :, :]).then_inc(signal, 16)

        def spread(ap):
            return ap.unsqueeze(2).to_broadcast([P, TPG, D])

        def over_tiles(ap):
            return ap.unsqueeze(1).to_broadcast([P, TPG, D])

        L0 = 0
        END_VAR = [3, 10, 15]
        END_STEPS = 17
        LOOPED = RING + 1
        LOOPS = (KEPT - LOOPED) // 2
        NORMED = GROUPS - 1
        SUMS0, STEPS0 = 6, 3 * LN_STEPS + 4
        SUMS1, STEPS1 = 2, LN_STEPS

        class Steps:

            def __init__(self, pool, base):
                self.pool, self.base, self.done = pool, base, 0

            def wait(self):
                self.done += 1
                self.pool.wait_ge(ln_steps, self.base + self.done)

            def __call__(self, out, a, b, op):
                nc.gpsimd.tensor_tensor(out, a, b, op).then_inc(ln_steps, 1)
                self.wait()

        def layer_norm(pool, step, src, sums_base, dst, after_mean=None, stored=None):
            pool.wait_ge(ln_sums, sums_base + 1)
            nc.gpsimd.tensor_tensor(ln_mean[:, :], ln_sum[:, :], neg_inv_d[:, :], ALU.mult).then_inc(ln_steps, 1)
            if after_mean:
                after_mean()
            step.wait()
            step(ln_c[:, :, :], src[:, :, :], spread(ln_mean[:, :]), ALU.add)
            pool.wait_ge(ln_sums, sums_base + 2)
            step(ln_var[:, :], ln_sum[:, :], inv_d[:, :], ALU.mult)
            step(ln_var[:, :], ln_var[:, :], eps_tile[:, :], ALU.add)
            step(ln_rstd[:, :], ln_var[:, :], minus_half[:, :], ALU.pow)
            if stored is not None:
                pool.wait_ge(ln_stored, stored)
            step(dst[:, :, :], ln_c[:, :, :], spread(ln_rstd[:, :]), ALU.mult)

        def edges_may_survive(eng):
            eng.wait_ge(flag_made, 1)
            return eng.value_load(flag[0:1, 0:1], min_val=0, max_val=1)

        STAGES = 9
        PROJECT, EDGES, ATTEND, COMPRESS, TURN_XN, PRUNE, NODES, GATHER, SCATTER = range(STAGES)
        SHARERS = 4
        CHUNKS = N // CH

        def meet(eng, l, stage):
            eng.drain().then_inc(gate, 1)
            eng.wait_ge(gate, (l * STAGES + (stage + 1)) * SHARERS)
            eng.sem_inc(passed, 1)


        def layer1_use(l):
            return Use((l + 1) * GROUPS, (l * GROUPS + KEPT) * CUTS, l * GROUPS + (1 + KEPT - LOOPED))

        def sp_score_rows(sp, l, k):
            with sp.Fori(0, T) as i:
                n = (l * 2 + k) * T + i
                sp.dma_start(h_rows[:, :], adj[bass.ds(i * P, P), :]).then_inc(h_loaded, 16)
                if k == 1:
                    sp.wait_ge(pruned_made, l * T + i + 1)
                    sp.dma_start(pruned[bass.ds(i * P, P), :], logits[:, :]).then_inc(pruned_stored, 16)
                sp.wait_ge(row_folded, n + 1)
                sp.sem_inc(passed, 1)

        def message_sp(sp):
            for dst, src in ((w_qv_sb[:, :], w_qv), (w_q_sb[:, :], w_q), (theta2[half(0), :], theta),
                             (theta2[half(1), :], theta), (b_q_sb[:, :], b_q),
                             (b_v_sb[:, :], b_v.partition_broadcast(P))):
                sp.dma_start(dst, src).then_inc(weights_loaded, 16)
            sp.wait_ge(weights_loaded, 16 * 6)
            with sp.Fori(0, ROUNDS) as l:
                meet(sp, l, PROJECT)
                meet(sp, l, EDGES)
                with sp.Fori(0, T // RING) as it:
                    load_rows(sp, adj, l * 2 + 1, it)
                meet(sp, l, ATTEND)
                sp_score_rows(sp, l, 0)
                meet(sp, l, COMPRESS)
                meet(sp, l, TURN_XN)
                meet(sp, l, PRUNE)
                sp_score_rows(sp, l, 1)
                sp.wait_ge(pruned_stored, (l + 1) * T * 16)
                sp.sem_inc(passed, 1)
                meet(sp, l, NODES)
                meet(sp, l, GATHER)
                with sp.Fori(0, T // RING) as it:
                    load_rows(sp, pruned, l * 2 + 2, it)
                meet(sp, l, SCATTER)
                with sp.Fori(0, GROUPS // 2) as it:
                    load_tiles(sp, pruned, layer1_use(l), it,
                               range(2 * CUTS))
            meet(sp, ROUNDS, PROJECT)

        def pe_score_rows(pe, l, k):
            moving = edge_t if k == 0 else xt_all
            with pe.Fori(0, T) as i:
                n = (l * 2 + k) * T + i
                pe.wait_ge(row_staged, n + 1)
                for c in range(CHUNKS):
                    if c >= 4:
                        pe.wait_ge(chunk_masked, n * CHUNKS + (c - 3))
                    pe.matmul(bank[c % 4][:, :], xt_tile[:, :], moving[:, CH * c:CH * c + CH],
                              start=True, stop=True).then_inc(chunk_scored, 1)
                if k == 0:
                    pe.wait_ge(recip_ready, n + 1)
                    for j in range(T):
                        mm = pe.matmul(bank[4][:, j:j + 1], logits[:, P * j:P * j + P], recip[:, :],
                                       start=True, stop=True)
                else:
                    pe.wait_ge(pruned_made, l * T + i + 1)
                    for b in range(BLOCKS):
                        for a in range(QUADS):
                            c0 = QCOLS * a + 32 * b
                            mm = pe.matmul(bank[4][32 * a:32 * a + 32, b:b + 1], logits[:, c0:c0 + 32],
                                           ones[:, 0:1], start=True, stop=True)
                mm.then_inc(row_folded, 1)

        def act_score_rows(act, l, k):
            with act.Fori(0, T) as i:
                n = (l * 2 + k) * T + i
                act.wait_ge(max_ready, n + 1)
                nc.scalar.activation(logits[:, :], logits[:, :], ACT.Exp, bias=neg_max[:, :],
                                     accum_out=part_sum[:, :]).then_inc(exp_ready, 1)

        def dve_score_rows(dve, l, k):
            with dve.Fori(0, T) as i:
                n = (l * 2 + k) * T + i
                nc.vector.tensor_copy(xt_tile[:, :], xt_all[:, bass.ds(i * P, P)]).then_inc(row_staged, 1)
                dve.wait_ge(h_loaded, (n + 1) * 16)
                for c in range(CHUNKS):
                    cs = slice(CH * c, CH * c + CH)
                    dve.wait_ge(chunk_scored, n * CHUNKS + (c + 1))
                    nc.vector.scalar_tensor_tensor(logits[:, cs], bank[c % 4][:, :], SCALE if k == 0 else 1.0,
                                                   h_rows[:, cs], ALU.mult, ALU.mult).then_inc(chunk_masked, 1)
                dve.wait_ge(chunk_masked, (n + 1) * CHUNKS)
                nc.vector.tensor_reduce(neg_max[:, :], logits[:, :], X, ALU.max, negate=True).then_inc(max_ready, 1)
                dve.wait_ge(exp_ready, n + 1)
                nc.vector.reciprocal(recip[:, :], part_sum[:, :]).then_inc(recip_ready, 1)
                if k == 0:
                    dve.wait_ge(row_folded, n + 1)
                    nc.vector.tensor_tensor(att[:, :], att[:, :], bank[4][:, 0:T], ALU.add).then_inc(edges_kept, 1)
                else:
                    dve.wait_ge(recip_ready, n + 1)
                    nc.vector.tensor_scalar(logits[:, :], logits[:, :], recip[:, :], threshold[:, :],
                                            ALU.mult, ALU.is_ge).then_inc(edges_kept, 1)
                    nc.vector.tensor_copy(mask_tile[:, :], comp_mask[:, bass.ds(i, 1)]).then_inc(mask_staged, 1)
                    dve.wait_ge(edges_kept, n + 1)
                    dve.wait_ge(mask_staged, l * T + i + 1)
                    nc.vector.scalar_tensor_tensor(logits[:, :], logits[:, :], mask_tile[:, :], h_rows[:, :],
                                                   ALU.mult, ALU.mult,
                                                   accum_out=conn_tile[:, :]).then_inc(pruned_made, 1)
                    dve.wait_ge(pruned_made, l * T + i + 1)
                    nc.vector.tensor_copy(conn[:, bass.ds(i, 1)], conn_tile[:, :])
                    dve.wait_ge(row_folded, n + 1)
                    nc.vector.tensor_tensor(edge_deg[:, :], edge_deg[:, :], bank[4][:, 0:BLOCKS],
                                            ALU.add).then_inc(row_added, 1)
                    dve.wait_ge(pruned_stored, (l * T + i + 1) * 16)
                    dve.wait_ge(row_added, l * T + i + 1)

        def node_chain(engine, l, stage):
            count, before = [0], 0 if stage == COMPRESS else COMPRESS_STEPS

            def step(who, make):
                if who is engine:
                    if count[0]:
                        engine.wait_ge(node_steps, l * (COMPRESS_STEPS + NODES_STEPS) + (before + count[0]))
                    make().then_inc(node_steps, 1)
                count[0] += 1

            v, a, p = nc.vector, nc.scalar, nc.tensor

            def tiles_of(ap):
                return ap.unsqueeze(2).to_broadcast([P, T, D])

            def sum_squares_of(src, dst):
                step(v, lambda: v.tensor_tensor(tmp, src, src, ALU.mult))
                step(v, lambda: v.tensor_reduce(dst, tmp, X, ALU.add))
                step(v, lambda: v.tensor_scalar(dst, dst, 1e-16, None, ALU.max))

            def softmax_mask(z, e, mask):
                step(v, lambda: v.tensor_reduce(part[:, :], z, X, ALU.max))
                step(v, lambda: v.tensor_scalar(diagonal[:, :], ident[:, :], part[:, :], None, ALU.mult))
                step(p, lambda: p.matmul(bank[0][:, 0:P], ones[:, :], diagonal[:, :], start=True, stop=True))
                step(v, lambda: v.tensor_reduce(neg_max[:, :], bank[0][:, 0:P], X, ALU.max, negate=True))
                step(a, lambda: a.activation(e, z, ACT.Exp, bias=neg_max[:, :], accum_out=part_sum[:, :]))
                step(p, lambda: p.matmul(bank[1][:, 0:1], ones[:, :], part_sum[:, :], start=True, stop=True))
                step(v, lambda: v.reciprocal(recip[:, :], bank[1][:, 0:1]))
                step(v, lambda: v.tensor_scalar(mask, e, recip[:, :], threshold[:, :], ALU.mult, ALU.is_ge))

            if stage == COMPRESS:
                sum_squares_of(xw_all[:, :, :], node_a[:, :])
                step(a, lambda: a.activation(node_b[:, :], node_a[:, :], ACT.Sqrt))
                step(v, lambda: v.tensor_scalar(att[:, :], att[:, :], 0.5 / N, None, ALU.mult))
                step(v, lambda: v.scalar_tensor_tensor(node_a[:, :], node_b[:, :], 0.5, att[:, :],
                                                       ALU.mult, ALU.add))
                softmax_mask(node_a[:, :], node_b[:, :], comp_mask[:, :])
                step(v, lambda: v.tensor_tensor(x_cur[:, :, :], x_cur[:, :, :], tiles_of(comp_mask[:, :]), ALU.mult))
                sum_squares_of(x_cur[:, :, :], node_a[:, :])
                step(a, lambda: a.activation(feat_mag[:, :], node_a[:, :], ACT.Sqrt))
                step(v, lambda: v.tensor_scalar(node_a[:, :], feat_mag[:, :], 1e-8, None, ALU.max))
                step(v, lambda: v.reciprocal(node_b[:, :], node_a[:, :]))
                step(v, lambda: v.tensor_tensor(rows_in[:, :, :], x_cur[:, :, :], tiles_of(node_b[:, :]), ALU.mult))
            else:
                step(v, lambda: v.tensor_tensor(node_a[:, :], conn[:, :], feat_mag[:, :], ALU.mult))
                softmax_mask(node_a[:, :], node_b[:, :], node_c[:, :])
                step(v, lambda: v.tensor_scalar(node_a[:, :], conn[:, :], 0.0, None, ALU.is_gt))
                step(v, lambda: v.tensor_tensor(node_c[:, :], node_c[:, :], node_a[:, :], ALU.mult))
                step(v, lambda: v.tensor_tensor(node_c[:, :], node_c[:, :], comp_mask[:, :], ALU.mult))
                step(v, lambda: v.tensor_scalar(node_a[:, :], conn[:, :], DEG_EPS, None, ALU.max))
                step(a, lambda: a.activation(node_b[:, :], node_a[:, :], ACT.Sqrt))
                step(v, lambda: v.reciprocal(dv[:, :], node_b[:, :]))
                step(v, lambda: v.tensor_tensor(node_c[:, :], node_c[:, :], dv[:, :], ALU.mult))
                step(v, lambda: v.tensor_tensor(rows_in[:, :, :], xw_all[:, :, :], tiles_of(node_c[:, :]), ALU.mult))
                step(v, lambda: v.tensor_scalar(edge_deg[:, :], edge_deg[:, :], DEG_EPS, None, ALU.max))
                step(v, lambda: v.reciprocal(node_a[:, :], edge_deg[:, :]))
            assert count[0] == (COMPRESS_STEPS if stage == COMPRESS else NODES_STEPS)

        COMPRESS_STEPS, NODES_STEPS = 22, 19

        def pe_turn_x(pe, l, k):
            with pe.Fori(0, T) as i:
                n = (l * 2 + k) * T + i
                pe.wait_ge(x_staged, n + 1)
                pe.transpose(bank[0][:, 0:P], x_pad[:, :], ident[:, :]).then_inc(x_turned, 1)
                if k == 0:
                    pe.wait_ge(xt_ready, n + 1)
                    pe.matmul(bank[1][:, 0:2 * D], xt_tile[:, :], w_qv_sb[:, :], start=True, stop=True)
                    pe.matmul(bank[2][0:D, 0:P], w_q_sb[:, :], xt_tile[:, :],
                              start=True, stop=True).then_inc(projected, 1)

        def message_pe(pe):
            with pe.Fori(0, ROUNDS) as l:
                meet(pe, l, PROJECT)
                pe_turn_x(pe, l, 0)
                meet(pe, l, EDGES)
                clear_sums(pe)
                with pe.Fori(0, T // RING) as it:
                    multiply_rows(pe, l * 2 + 1, it)
                meet(pe, l, ATTEND)
                pe_score_rows(pe, l, 0)
                meet(pe, l, COMPRESS)
                node_chain(pe, l, COMPRESS)
                meet(pe, l, TURN_XN)
                pe_turn_x(pe, l, 1)
                meet(pe, l, PRUNE)
                pe_score_rows(pe, l, 1)
                meet(pe, l, NODES)
                node_chain(pe, l, NODES)
                meet(pe, l, GATHER)
                clear_sums(pe)
                with pe.Fori(0, T // RING) as it:
                    multiply_rows(pe, l * 2 + 2, it)
                pe.wait_ge(cols_copied, l * 2 + 4)
                pe.sem_inc(passed, 1)
                for b in range(BANKS):
                    turn_cols(pe, b, bank[b])
                meet(pe, l, SCATTER)
                with pe.Fori(0, GROUPS // 2) as it:
                    multiply_tiles(pe, layer1_use(l), it, theta2, CUTS - 1)
            meet(pe, ROUNDS, PROJECT)

        def act_turn_x(act, l, k):
            with act.Fori(0, T) as i:
                n = (l * 2 + k) * T + i
                act.wait_ge(x_turned, n + 1)
                if k == 0:
                    act.copy(xt_tile[:, :], bank[0][0:D, 0:P]).then_inc(xt_ready, 1)
                    act.wait_ge(projected, l * T + i + 1)
                    nc.scalar.activation(xt_all[:, bass.ds(i * P, P)], bank[2][0:D, 0:P], ACT.Identity,
                                         bias=b_q_sb[:, :]).then_inc(q_kept, 1)
                else:
                    act.copy(xt_all[:, bass.ds(i * P, P)], bank[0][0:D, 0:P]).then_inc(xt_ready, 1)

        def message_act(act):
            with act.Fori(0, ROUNDS) as l:
                meet(act, l, PROJECT)
                act_turn_x(act, l, 0)
                meet(act, l, EDGES)
                with act.Fori(0, T // RING) as it:
                    stage_rows(act, l * 2 + 1, it)
                act.wait_ge(rows_used, (l * 2 + 2) * T)
                for b in range(BANKS):
                    for h in range(2):
                        c0 = HALF * h + CH * b
                        act.copy(edge_t[:, c0:c0 + CH], bank[b][half(h), :])
                meet(act, l, ATTEND)
                act_score_rows(act, l, 0)
                meet(act, l, COMPRESS)
                node_chain(act, l, COMPRESS)
                meet(act, l, TURN_XN)
                act_turn_x(act, l, 1)
                meet(act, l, PRUNE)
                act_score_rows(act, l, 1)
                meet(act, l, NODES)
                node_chain(act, l, NODES)
                meet(act, l, GATHER)
                with act.Fori(0, T // RING) as it:
                    stage_rows(act, l * 2 + 2, it)
                act.wait_ge(rows_used, (l * 2 + 3) * T)
                for h in range(2):
                    copy_cols(act, h)
                meet(act, l, SCATTER)
                with act.Fori(0, GROUPS // 2) as it:
                    for k in range(2):
                        act.wait_ge(tiles_used, (it * 2 + (l * GROUPS + (KEPT + k + 1))) * CUTS)
                        copy_sums(act.copy, k)
            meet(act, ROUNDS, PROJECT)
            act.wait_ge(msg_added, 1)
            with act.Fori(0, GROUPS) as g:
                p0 = g * STEPS1 + NORMED * STEPS0
                for t in range(TPG):
                    last = nc.scalar.activation(ln_h[:, t, :], x_cur[:, bass.ds(g * TPG + t, 1), :].squeeze(1),
                                                ACT.Copy, accum_out=ln_sum[:, t:t + 1])
                last.then_inc(ln_sums, 1)
                act.wait_ge(ln_steps, p0 + 2)
                sum_squares(act)
                act.wait_ge(ln_steps, p0 + STEPS1)
                store_group(act, g, ln_out, ln_stored)
            act.wait_ge(ln_stored, 16 * (NORMED + GROUPS + 1))

        def dve_turn_x(dve, l, k):
            src = x_cur if k == 0 else rows_in
            with dve.Fori(0, T) as i:
                n = (l * 2 + k) * T + i
                nc.vector.tensor_copy(x_pad[:, 0:D], src[:, bass.ds(i, 1), :].squeeze(1)).then_inc(x_staged, 1)
                if k == 0:
                    m = l * T + i + 1
                    dve.wait_ge(projected, m)
                    nc.vector.tensor_copy(xw_all[:, bass.ds(i, 1), :].squeeze(1), bank[1][:, 0:D])
                    nc.vector.tensor_tensor(rows_in[:, bass.ds(i, 1), :].squeeze(1), bank[1][:, D:2 * D],
                                            b_v_sb[:, :], ALU.add).then_inc(row_kept, 1)
                    dve.wait_ge(q_kept, m)
                    dve.wait_ge(row_kept, m)
                else:
                    dve.wait_ge(xt_ready, n + 1)

        def message_dve(dve):
            dve.wait_ge(ln_stored, 16 * (NORMED + 1))
            dve.wait_ge(end_steps, END_STEPS)
            nc.vector.tensor_copy(x_cur[:, :, :], x_all[:, :, :])
            nc.vector.memset(ones[:, :], 1.0)
            nc.vector.memset(x_pad[:, :], 0.0)
            for r in range(ROUNDS):
                nc.vector.memset(thresholds[:, r:r + 1], THETA[r])
            with dve.Fori(0, ROUNDS) as l:
                meet(dve, l, PROJECT)
                nc.vector.tensor_copy(threshold[:, :], thresholds[:, bass.ds(l, 1)])
                nc.vector.memset(att[:, :], 0.0)
                nc.vector.memset(edge_deg[:, :], 0.0)
                dve_turn_x(dve, l, 0)
                nc.vector.memset(zeros[:, :], 0.0)
                meet(dve, l, EDGES)
                meet(dve, l, ATTEND)
                dve_score_rows(dve, l, 0)
                meet(dve, l, COMPRESS)
                node_chain(dve, l, COMPRESS)
                meet(dve, l, TURN_XN)
                dve_turn_x(dve, l, 1)
                meet(dve, l, PRUNE)
                dve_score_rows(dve, l, 1)
                meet(dve, l, NODES)
                node_chain(dve, l, NODES)
                nc.vector.memset(zeros[:, :], 0.0)
                meet(dve, l, GATHER)
                for b in range(BANKS):
                    dve.wait_ge(cols_turned, (l + 1) * BANKS + (b + 1))
                    nc.vector.tensor_tensor(cols[:, 8 * b:8 * b + 8, :],
                                            bank[b][:, :].rearrange("p (t d) -> p t d", d=D),
                                            node_a[:, 8 * b:8 * b + 8].unsqueeze(2).to_broadcast([P, 8, D]), ALU.mult)
                meet(dve, l, SCATTER)
                with dve.Fori(0, GROUPS // 2) as it:
                    for k in range(2):
                        turn_tiles(dve, layer1_use(l), it,
                                   range(k * CUTS, k * CUTS + CUTS))
                        g = it * 2 + k
                        dve.wait_ge(nat_ready, g + (l * GROUPS + (GROUPS + 1)))
                        nc.vector.tensor_tensor(ln_c[:, :, :], nat_bank[k][:, 0:TPG * D].rearrange("p (t d) -> p t d", d=D),
                                                dv[:, bass.ds(g * TPG, TPG)].unsqueeze(2).to_broadcast([P, TPG, D]),
                                                ALU.mult).then_inc(nat_read, 1)
                        dve.wait_ge(nat_read, g + (l * GROUPS + (GROUPS + 3)))
                        nc.vector.tensor_scalar(x_cur[:, bass.ds(g * TPG, TPG), :], ln_c[:, :, :], 0.0, None,
                                                ALU.max).then_inc(msg_kept, 1)
                        dve.wait_ge(msg_kept, g + (l * GROUPS + 1))
            meet(dve, ROUNDS, PROJECT)
            nc.vector.tensor_tensor(x_cur[:, :, :], x_cur[:, :, :], x_all[:, :, :], ALU.add).then_inc(msg_added, 1)

        def message_pool(pool):
            pool.wait_ge(gate, (ROUNDS * STAGES + 1) * SHARERS)
            with pool.Fori(0, GROUPS) as g:
                step = Steps(pool, g * STEPS1 + NORMED * STEPS0)
                layer_norm(pool, step, ln_h, g * SUMS1 + NORMED * SUMS0, ln_out,
                           stored=(g + (NORMED + 1)) * 16)

        loop_use = Use(LOOPED + 1, LOOPED * CUTS, 1, LOOPED)

        @block.sync
        def _(sp):
            sp.dma_start(x_all[:, :, :], x.rearrange("(t p) d -> p t d", p=P)).then_inc(x_loaded, 16)
            for h in range(2):
                sp.dma_start(w_ui_sb[half(h), :], w_ui).then_inc(const_loaded, 16)
            sp.dma_start(diag_sb[:, :], diag).then_inc(const_loaded, 16)
            sp.dma_start(par_sb[:, :], par.partition_broadcast(P)).then_inc(const_loaded, 16)
            load_rows(sp, adj, L0, 0, first=True)
            with sp.Fori(1, T // RING) as it:
                load_rows(sp, adj, L0, it)
            def load_spare(g, q, turned_before):
                if turned_before is not None:
                    sp.wait_ge(halves_turned, turned_before * 2)
                load_tile(sp, adj, RING + q % SPARE, g, q, [spare_loaded[q % SPARE]])

            for q in range(CUTS):
                load_spare(0, q, q - SPARE + 1 if q >= SPARE else None)
            with sp.Fori(1, RING) as g:
                for q in range(CUTS):
                    load_spare(g, q, g * CUTS + (q - SPARE + 1))
            sp.wait_ge(rows_scanned, T)
            for u in range(RING):
                sp.wait_ge(blocks_flipped, (u + 1) * FLIPS)
                load_tile(sp, adj, u, RING, u, [tiles_loaded[u]])
            with sp.Fori(0, LOOPS - 1) as it:
                load_tiles(sp, adj, loop_use, it, range(2 * CUTS))
            load_tiles(sp, adj, loop_use, LOOPS - 1, range(2 * CUTS), end=True)
            sp.wait_ge(end_steps, END_STEPS)
            store_group(sp, KEPT - 1, end_y, end_stored)
            sp.wait_ge(end_stored, 16)
            with sp.If(edges_may_survive(sp) > 0):
                message_sp(sp)

        @block.gpsimd
        def _(pool):
            nc.gpsimd.memset(ident[:, :], 0.0).then_inc(ident_clear, 1)
            nc.gpsimd.memset(stack[:, :], 0.0).then_inc(ident_clear, 1)
            for tile, value in ((minus_half, -0.5), (inv_d, 1.0 / D), (neg_inv_d, -1.0 / D), (eps_tile, LN_EPS)):
                nc.gpsimd.memset(tile[:, :], value).then_inc(ident_clear, 1)
            pool.wait_ge(ident_clear, 6)
            nc.gpsimd.affine_select(out=ident[:, :], in_=ident[:, :], compare_op=ALU.not_equal, fill=1.0,
                                    base=0, pattern=[[-1, P]], channel_multiplier=1).then_inc(const_made, 1)
            for h in range(2):
                pool.wait_ge(const_made, 1 + h)
                nc.gpsimd.affine_select(out=stack[:, :], in_=stack[:, :], compare_op=ALU.not_equal, fill=1.0,
                                        base=-D * h, pattern=[[-1, D]],
                                        channel_multiplier=1).then_inc(const_made, 1)
            pool.wait_ge(max_found, 1)
            nc.gpsimd.partition_all_reduce(all_max[:, :], part_max[:, :], P, bass.bass_isa.ReduceOp.max).then_inc(max_found, 1)
            pool.wait_ge(max_found, 2)
            nc.gpsimd.tensor_scalar(flag[:, :], all_max[:, :], LIMIT, None, ALU.is_ge).then_inc(flag_made, 1)

            pool.sem_inc(ln_stored, 16)
            pool.wait_ge(small_loaded, 16 * 2)
            def finish_group(count, tiles):
                s0 = count * SUMS0
                step = Steps(pool, count * STEPS0)
                layer_norm(pool, step, ln_h, s0, ln_y,
                           after_mean=lambda: nc.gpsimd.tensor_copy(ln_x[:, :, :], x_all[:, tiles, :]))
                step(ln_y[:, :, :], ln_y[:, :, :], over_tiles(gamma_sb[:, :]), ALU.mult)
                step(ln_y[:, :, :], ln_y[:, :, :], over_tiles(beta_sb[:, :]), ALU.add)
                step(ln_y[:, :, :], ln_y[:, :, :], ln_x[:, :, :], ALU.add)
                step(ln_h[:, :, :], ln_y[:, :, :], ln_x[:, :, :], ALU.add)
                layer_norm(pool, step, ln_h, s0 + 2, ln_y)
                layer_norm(pool, step, ln_y, s0 + 4, ln_out, stored=(count + 1) * 16,
                           after_mean=lambda: nc.gpsimd.tensor_copy(x_all[:, tiles, :], ln_y[:, :, :]))

            with pool.Fori(0, RING) as m:
                finish_group(m, bass.ds(m * TPG, TPG))
            finish_group(RING, slice(KEPT * TPG, T))
            tiles = slice((KEPT - 1) * TPG, KEPT * TPG)
            nc.gpsimd.tensor_tensor(end_add[:, :, :], x_all[:, tiles, :], over_tiles(beta_sb[:, :]),
                                    ALU.add).then_inc(add_made, 1)
            pool.wait_ge(add_made, 1)
            nc.gpsimd.tensor_tensor(end_add[:, :, :], end_add[:, :, :], x_all[:, tiles, :],
                                    ALU.add).then_inc(add_made, 1)
            with pool.Fori(RING + 1, NORMED) as m:
                finish_group(m, bass.ds((m - 1) * TPG, TPG))
            for n in range(3):
                pool.wait_ge(end_steps, END_VAR[n])
                nc.gpsimd.tensor_tensor(end_rstd[:, :], end_var[:, :], minus_half[:, :],
                                        ALU.pow).then_inc(end_steps, 1)
            with pool.If(edges_may_survive(pool) > 0):
                message_pool(pool)

        @block.scalar
        def _(act):
            act.dma_start(gamma_sb[:, :], gamma.partition_broadcast(P)).then_inc(small_loaded, 16)
            act.dma_start(beta_sb[:, :], beta.partition_broadcast(P)).then_inc(small_loaded, 16)
            for b in range(BANKS):
                act.wait_ge(pairs_turned, b + 1)
                act.copy(xt_pairs[:, CH * b:CH * b + CH], bank[b % 4][:, :]).then_inc(pairs_copied, 1)
            act.wait_ge(e_made, 1)
            stage_rows(act, L0, 0, first=True)
            act.wait_ge(e_made, BANKS)
            with act.Fori(1, T // RING) as it:
                stage_rows(act, L0, it)
            act.wait_ge(rows_used, T)
            copy_cols(act, 0)
            copy_cols(act, 1)
            for b in range(BANKS):
                act.wait_ge(cols_turned, b + 1)
                act.copy(cols[:, 8 * b:8 * b + 8, :],
                         bank[b][:, :].rearrange("p (t d) -> p t d", d=D)).then_inc(cols_made, 1)
            act.wait_ge(cols_made, BANKS)
            make_cols_nat(act)

            def sum_part(count, g, part, nat):
                p0, s0 = count * STEPS0, count * SUMS0
                if part == 0:
                    act.wait_ge(nat_ready, count + 1)
                    for t in range(TPG):
                        last = nc.scalar.activation(ln_h[:, t, :], nat_bank[nat][:, D * t:D * t + D], ACT.Copy,
                                                    accum_out=ln_sum[:, t:t + 1])
                    last.then_inc(ln_sums, 1)
                    act.wait_ge(ln_sums, s0 + 1)
                    act.sem_inc(nat_read, 1)
                    act.wait_ge(ln_steps, p0 + 2)
                    sum_squares(act)
                elif part < 3:
                    act.wait_ge(ln_steps, p0 + (LN_STEPS + 4 if part == 1 else 2 * LN_STEPS + 4))
                    sum_features(act, ln_h if part == 1 else ln_y)
                    act.wait_ge(ln_steps, p0 + (LN_STEPS + 6 if part == 1 else 2 * LN_STEPS + 6))
                    sum_squares(act)
                else:
                    act.wait_ge(ln_steps, p0 + STEPS0)
                    store_group(act, g, ln_out, ln_stored)

            for n in range(EARLY):
                copy_flipped(act, n)
                g, q = n // CUTS, n % CUTS
                if q and g >= 1:
                    sum_part(g - 1, g - 1, q - 1, (g - 1) % 2)
                elif q == 0 and g >= 2:
                    sum_part(g - 2, g - 2, 3, g % 2)
            sum_part(RING - 2, RING - 2, 3, 0)
            for part in range(4):
                sum_part(RING - 1, RING - 1, part, 1)
            for part in range(4):
                sum_part(RING, KEPT, part, 0)
            with act.Fori(0, (NORMED - RING - 1) // 2) as it:
                for k in range(2):
                    for part in range(4):
                        sum_part(it * 2 + (RING + 1 + k), it * 2 + (RING + k), part, (RING + 1 + k) % 2)
            act.wait_ge(ln_stored, 16 * (NORMED + 1))
            with act.If(edges_may_survive(act) > 0):
                message_act(act)

        @block.vector
        def _(dve):
            dve.wait_ge(const_loaded, 16 * 4)
            nc.vector.tensor_tensor(pp[:, :], par_sb[:, 0:4:2], par_sb[:, 1:4:2], ALU.mult).then_inc(pp_made, 1)
            dve.wait_ge(pp_made, 1)
            for k, (a, b) in enumerate(((0, USER_TILES), (USER_TILES, T))):
                nc.vector.tensor_scalar(diag_sb[:, a:b], diag_sb[:, a:b], pp[:, k:k + 1], None,
                                        ALU.mult).then_inc(pp_made, 1)
            dve.wait_ge(pp_made, 3)
            dve.wait_ge(x_loaded, 16)
            for b in range(BANKS):
                dve.wait_ge(xw_done, b + 1)
                for odd in range(2):
                    tiles = slice(8 * b + odd, 8 * b + 8, 2)
                    scaled = nc.vector.tensor_tensor(rows_in[:, tiles, :], xw_out(b, odd),
                                                     diag_sb[:, tiles].unsqueeze(2).to_broadcast([P, 4, D]), ALU.mult)
                scaled.then_inc(e_scaled, 1)
                dve.wait_ge(e_scaled, b + 1)
                t8 = slice(8 * b, 8 * b + 8)
                nc.vector.tensor_tensor(rows_in[:, t8, :], rows_in[:, t8, :], x_all[:, t8, :],
                                        ALU.add).then_inc(e_made, 1)
            with dve.Fori(0, T // RING) as it:
                for s in range(RING):
                    dve.wait_ge(rows_loaded[s], (it + 1) * 16)
                    nc.vector.tensor_reduce(row_max[:, bass.ds(it * RING + s, 1)], ring[s][:, :], X, ALU.max,
                                            apply_absolute_value=True).then_inc(rows_scanned, 1)
            dve.wait_ge(rows_scanned, T)
            nc.vector.tensor_reduce(part_max[:, :], row_max[:, :], X, ALU.max).then_inc(max_found, 1)
            def turn_spare(n, q):
                dve.wait_ge(spare_loaded[q % SPARE], (n // SPARE + 1) * 64)
                turn_tile(RING + q % SPARE, turned[q % 2])

            turn_spare(0, 0)
            dve.wait_ge(cols_turned, BANKS)
            turn_spare(1, 1)
            for q in range(2, CUTS):
                dve.wait_ge(tiles_used, q - 1)
                turn_spare(q, q)
            for g in range(1, RING):
                for q in range(CUTS):
                    n = g * CUTS + q
                    dve.wait_ge(tiles_used, n - 1)
                    turn_spare(n, q)
                    if q == 0:
                        dve.wait_ge(tiles_used, n)
                        copy_sums(nc.vector.tensor_copy, (g - 1) % 2)
            for q in range(CUTS):
                n = EARLY + q
                dve.wait_ge(tiles_loaded[q], 64)
                dve.wait_ge(tiles_used, n - 1)
                turn_tile(q, turned[q % 2])
                if q == 0:
                    dve.wait_ge(tiles_used, EARLY)
                    copy_sums(nc.vector.tensor_copy, 1)
                elif q == 1:
                    dve.wait_ge(flipped_used, STEPS)
                    copy_sums(nc.vector.tensor_copy, 0, kept_bank)

            def turn_groups(it, end=False):
                for k in range(2):
                    turn_tiles(dve, loop_use, it, range(k * CUTS, k * CUTS + 1))
                    dve.wait_ge(tiles_used, it * (2 * CUTS) + (LOOPED + k) * CUTS)
                    copy_sums(nc.vector.tensor_copy, (LOOPED - 1 + k) % 2)
                    turn_tiles(dve, loop_use, it, range(k * CUTS + 1, k * CUTS + CUTS), end=end and k == 1)

            with dve.Fori(0, LOOPS - 1) as it:
                turn_groups(it)
            turn_groups(LOOPS - 1, end=True)
            dve.wait_ge(tiles_used, KEPT * CUTS)
            copy_sums(nc.vector.tensor_copy, (KEPT - 1) % 2)

            done = [0]

            def end_step(ins):
                done[0] += 1
                ins.then_inc(end_steps, 1)

            def end_norm(src, dst, n):
                for t in range(TPG):
                    stats = nc.vector.bn_stats(end_stats[:, t, :], src(t))
                end_step(stats)
                dve.wait_ge(end_steps, done[0])
                for t in range(TPG):
                    mv = nc.vector.bn_aggr(end_mv[:, t, :], end_stats[:, t, :])
                end_step(mv)
                dve.wait_ge(end_steps, done[0])
                end_step(nc.vector.tensor_scalar(end_var[:, :], end_mv[:, :, 1], LN_EPS, None, ALU.add))
                assert done[0] == END_VAR[n]
                done[0] += 1
                dve.wait_ge(end_steps, done[0])
                for t in range(TPG):
                    y = nc.vector.tensor_scalar(dst(t), src(t), end_mv[:, t, 0:1], end_rstd[:, t:t + 1],
                                                ALU.subtract, ALU.mult)
                end_step(y)
                dve.wait_ge(end_steps, done[0])

            dve.wait_ge(nat_ready, GROUPS)
            end_norm(lambda t: nat_bank[1][:, D * t:D * t + D], lambda t: end_y[:, t, :], 0)
            dve.sem_inc(nat_read, 1)
            end_step(nc.vector.tensor_tensor(end_y[:, :, :], end_y[:, :, :], over_tiles(gamma_sb[:, :]), ALU.mult))
            dve.wait_ge(end_steps, done[0])
            dve.wait_ge(add_made, 2)
            end_step(nc.vector.tensor_tensor(end_y[:, :, :], end_y[:, :, :], end_add[:, :, :], ALU.add))
            dve.wait_ge(end_steps, done[0])
            x1_tile = (KEPT - 1) * TPG
            end_norm(lambda t: end_y[:, t, :], lambda t: x_all[:, x1_tile + t, :], 1)
            end_norm(lambda t: x_all[:, x1_tile + t, :], lambda t: end_y[:, t, :], 2)
            assert done[0] == END_STEPS
            with dve.If(edges_may_survive(dve) > 0):
                message_dve(dve)

        @block.tensor
        def _(pe):
            pe.sem_inc(nat_read, 2)
            pe.wait_ge(x_loaded, 16)
            pe.wait_ge(const_made, 3)

            def turn_pairs(b):
                if b >= 4:
                    pe.wait_ge(pairs_copied, b - 3)
                for j in range(4):
                    t = 8 * b + 2 * j
                    mm = pe.transpose(bank[b % 4][:, P * j:P * j + P],
                                      x_all[:, t:t + 2, :].rearrange("p t d -> p (t d)"), ident[:, :])
                mm.then_inc(pairs_turned, 1)

            for b in range(4):
                turn_pairs(b)
            pe.wait_ge(const_loaded, 16 * 4)
            for b in range(BANKS):
                pe.wait_ge(pairs_copied, b + 1)
                if b >= 2:
                    pe.wait_ge(e_scaled, b - 1)
                for t in range(8 * b, 8 * b + 8):
                    odd, k = t % 2, 0 if t < USER_TILES else 1
                    mm = pe.matmul(xw_out(b, odd)[:, t % 8 // 2, :], xt_pairs[half(odd), P * (t // 2):P * (t // 2) + P],
                                   w_ui_sb[half(odd), D * k:D * k + D], start=True, stop=True)
                mm.then_inc(xw_done, 1)
                if b == 0:
                    turn_pairs(4)
            pe.wait_ge(e_made, BANKS)
            multiply_rows(pe, L0, 0, first=True)
            with pe.Fori(1, T // RING) as it:
                multiply_rows(pe, L0, it)
            pe.wait_ge(cols_copied, 2)
            for b in range(BANKS):
                turn_cols(pe, b, bank[b])
            pe.wait_ge(cols_made, BANKS)
            for n in range(LOOPED * CUTS):
                g, q = n // CUTS, n % CUTS
                multiply_tile(pe, n, g % 2, q)
                if q == 0 and g:
                    close_group(pe, g - 1, (g - 1) % 2, (g - 1) % 2, stack[:, :])
                if n == 2:
                    pe.wait_ge(cols_nat_ready, 1)
                if 2 <= n <= EARLY:
                    multiply_flipped(pe, n - 1)
                if n < EARLY:
                    flip_blocks(pe, n)
                if n == EARLY + 1:
                    close_group(pe, RING, 0, 0, stack[:, :])
            with pe.Fori(0, LOOPS) as it:
                multiply_tiles(pe, loop_use, it, stack[:, :], 0)
            close_group(pe, GROUPS - 1, 0, 1, stack[:, :])
            with pe.If(edges_may_survive(pe) > 0):
                message_pe(pe)


_INS = ("x", "adj", "w_ui", "diag", "par", "gamma", "beta", "w_qv", "w_q", "theta", "b_q", "b_v")


def kernel(**inputs):
    import numpy as np
    import concourse.bacc as bacc
    from concourse.bass_utils import run_bass_kernel_spmd as run

    a = {k: np.asarray(v) for k, v in inputs.items()}
    laid = {
        "x": a["x"],
        "adj": a["adj"],
        "w_ui": np.concatenate([a["L0_gnn_W_u"], a["L0_gnn_W_i"]], axis=1),
        "diag": np.ascontiguousarray(np.concatenate([a["L0_gnn_diag_u"], a["L0_gnn_diag_i"]]).reshape(-1, 128).T),
        "par": np.concatenate([a["L0_gnn_par_u"], a["L0_gnn_par_i"]]),
        "gamma": a["L0_gnn_ln_gamma"],
        "beta": a["L0_gnn_ln_beta"],
        "w_qv": np.concatenate([a["L1_gnn_W"], a["L1_gnn_Wv"]], axis=1),
        "w_q": a["L1_gnn_Wq"],
        "theta": a["L1_gnn_Theta"],
        "b_q": a["L1_gnn_bq"].reshape(-1, 1),
        "b_v": a["L1_gnn_bv"],
    }
    nc = bacc.Bacc("TRN2", target_bir_lowering=False, num_devices=1)
    arrays, args = {}, []
    for name in _INS:
        v = np.ascontiguousarray(laid[name])
        arrays[f"in_{name}"] = v
        args.append(nc.dram_tensor(f"in_{name}", v.shape, mybir.dt.from_np(v.dtype), kind="ExternalInput").ap())
    shape = a["x"].shape
    args.append(nc.dram_tensor("out_0", shape, mybir.dt.from_np(a["x"].dtype), kind="ExternalOutput").ap())
    adjacency_layers_kernel(nc, *args)
    r = run(nc, [arrays], core_ids=[0])
    return r.results[0]["out_0"]
```

```python
import math
from contextlib import ExitStack

import concourse.bass as bass
from concourse import mybir


def adjacency_layers_kernel(nc, x, adj, w_ui, diag, par, gamma, beta,
                            w_qv, w_q, theta, b_q, b_v, out):
    f32 = mybir.dt.float32
    i32 = mybir.dt.int32
    ALU = mybir.AluOpType
    ACT = mybir.ActivationFunctionType
    X = mybir.AxisListType.X

    P = 128
    N, D = x.shape
    T = N // P
    USER_TILES = 2048 // P
    CH = 512
    BANKS = N // (2 * CH)
    HALF = N // 2
    RING = 4
    SPARE = 2
    QUADS = 4
    QCOLS = N // QUADS
    BLOCKS = QCOLS // 32
    CUTS = 4
    BPT = BLOCKS // CUTS
    GROUP = 512
    GROUPS = N // GROUP
    TPG = GROUP // P
    RSUB = GROUP // 32
    KEPT = GROUPS - 1
    FLIPS = T // 4
    FLIP_STEPS = RING * FLIPS
    EARLY = RING * CUTS
    BURST = -(-FLIP_STEPS // (EARLY - 1))
    LN_EPS = 1e-5
    DEG_EPS = 1e-6
    SCALE = float(D) ** -0.5
    ROUNDS = 2
    THETA = [0.000244 + (1.0 - math.exp(-0.1 * it)) * (0.0003 - 0.000244) for it in range(ROUNDS)]
    LIMIT = 0.5 * math.log(N * THETA[0]) - 0.01

    pruned = nc.dram_tensor("pruned_adjacency", [N, N], f32, kind="Internal").ap()

    ctx = ExitStack()
    with ctx:
        def sb(name, shape, dt=f32):
            return ctx.enter_context(nc.sbuf_tensor(name, shape, dt))

        def sem(name):
            return ctx.enter_context(nc.semaphore(name))

        ring = [sb(f"ring{s}", [P, N]) for s in range(RING + SPARE)]
        turned = [sb(f"turned{s}", [P, N]) for s in range(2)]
        x_all = sb("x_all", [P, T, D])
        rows_in = sb("rows_in", [P, T, D])
        cols = sb("cols", [P, BLOCKS, D])
        sums = [sb(f"sums{s}", [P, GROUP]) for s in range(2)]
        flipped = [sb(f"flipped{s}", [P, CH]) for s in range(BURST)]
        staged = [flipped[1][:, TPG * D + D * s:TPG * D + D * s + D] for s in range(RING)]
        ident = sb("ident", [P, P])
        stack = sb("stack", [P, D])
        zeros = sums[0]
        w_ui_sb = sb("w_ui_sb", [P, 2 * D])
        diag_sb = sb("diag_sb", [P, T])
        par_sb = sb("par_sb", [P, 4])
        pp = sb("pp", [P, 2])
        gamma_sb = sb("gamma_sb", [P, D])
        beta_sb = sb("beta_sb", [P, D])
        row_max = sb("row_max", [P, T])
        part_max = sb("part_max", [P, 1])
        all_max = sb("all_max", [P, 1])
        flag = sb("flag", [P, 1], i32)
        ln_h = sb("ln_h", [P, TPG, D])
        ln_c = sb("ln_c", [P, TPG, D])
        ln_y = sb("ln_y", [P, TPG, D])
        ln_sum = sb("ln_sum", [P, TPG])
        ln_mean = sb("ln_mean", [P, TPG])
        ln_var = sb("ln_var", [P, TPG])
        ln_rstd = sb("ln_rstd", [P, TPG])
        ln_out = sb("ln_out", [P, TPG, D])
        ln_x = sb("ln_x", [P, TPG, D])
        minus_half = sb("minus_half", [P, TPG])
        inv_d = sb("inv_d", [P, TPG])
        neg_inv_d = sb("neg_inv_d", [P, TPG])
        eps_tile = sb("eps_tile", [P, TPG])
        end_stats = sb("end_stats", [P, TPG, 6])
        end_mv = sb("end_mv", [P, TPG, 2])
        end_var = sb("end_var", [P, TPG])
        end_rstd = sb("end_rstd", [P, TPG])
        end_y, end_add = [flipped[i][:, 0:TPG * D].rearrange("p (t d) -> p t d", d=D)
                          for i in range(2)]

        cols_t = turned[1][0:D, :]
        cols_nat = rows_in

        xt_pairs = turned[0][:, 0:T // 2 * P]

        carved = [T * D]

        def carve(width, parts=P):
            carved[0] += width
            return ring[RING][0:parts, carved[0] - width:carved[0]]

        x_cur = ring[RING][:, 0:T * D].rearrange("p (t d) -> p t d", d=D)
        w_qv_sb = carve(2 * D, D)
        w_q_sb = carve(D, D)
        theta2 = carve(D)
        b_q_sb = carve(1, D)
        b_v_sb = carve(D)
        thresholds = carve(ROUNDS)
        threshold = carve(1)
        x_pad = carve(P)
        xt_tile = carve(P, D)
        ones = carve(P)
        diagonal = carve(P)
        node_a, node_b, node_c = carve(T), carve(T), carve(T)
        att = carve(T)
        comp_mask = carve(T)
        feat_mag = carve(T)
        conn = carve(T)
        edge_deg = carve(BLOCKS)
        dv = carve(T)
        part, neg_max, part_sum, recip, mask_tile, conn_tile = (carve(1) for _ in range(6))

        xt_all = turned[0][0:D, :]
        edge_t = turned[1][0:D, :]
        h_rows, logits = ring[0], ring[1]
        tmp = ring[2][:, 0:T * D].rearrange("p (t d) -> p t d", d=D)
        xw_all = cols

        bank = [ctx.enter_context(nc.psum_tensor(f"bank{b}", [P, CH], f32)) for b in range(8)]
        sum_bank = [bank[5], bank[6]]
        nat_bank = [bank[0], bank[7]]
        kept_bank = bank[4]
        flip_bank = [bank[1 + i] for i in range(BURST)]

        const_loaded = sem("const_loaded")
        x_loaded = sem("x_loaded")
        const_made = sem("const_made")
        ident_clear = sem("ident_clear")
        pp_made = sem("pp_made")
        pairs_turned = sem("pairs_turned")
        pairs_copied = sem("pairs_copied")
        xw_done = sem("xw_done")
        e_scaled = sem("e_scaled")
        e_made = sem("e_made")
        rows_loaded = [sem(f"rows_loaded{s}") for s in range(RING)]
        tile_staged = sem("tile_staged")
        rows_used = sem("rows_used")
        rows_scanned = sem("rows_scanned")
        cols_copied = sem("cols_copied")
        cols_turned = sem("cols_turned")
        tiles_loaded = [sem(f"tiles_loaded{s}") for s in range(RING)]
        halves_turned = sem("halves_turned")
        end_loaded = [sem(f"end_loaded{i}") for i in range(2)]
        end_turned = sem("end_turned")
        end_multiplied = sem("end_multiplied")
        end_copied = sem("end_copied")
        end_closed = sem("end_closed")
        spare_loaded = [sem(f"spare_loaded{s}") for s in range(SPARE)]
        cols_made = sem("cols_made")
        cols_nat_ready = sem("cols_nat_ready")
        blocks_flipped = sem("blocks_flipped")
        blocks_copied = sem("blocks_copied")
        flipped_used = sem("flipped_used")
        add_made = sem("add_made")
        end_steps = [sem(f"end_steps{h}") for h in range(2)]
        end_stored = sem("end_stored")
        tiles_used = sem("tiles_used")
        sums_copied = sem("sums_copied")
        nat_ready = sem("nat_ready")
        nat_read = sem("nat_read")
        ln_sums = sem("ln_sums")
        ln_steps = sem("ln_steps")
        ln_stored = sem("ln_stored")
        max_found = sem("max_found")
        flag_made = sem("flag_made")
        weights_loaded = sem("weights_loaded")
        gate = sem("gate")
        passed = sem("passed")
        x_staged = sem("x_staged")
        x_turned = sem("x_turned")
        xt_ready = sem("xt_ready")
        projected = sem("projected")
        q_kept = sem("q_kept")
        h_loaded = sem("h_loaded")
        row_staged = sem("row_staged")
        chunk_scored = sem("chunk_scored")
        chunk_masked = sem("chunk_masked")
        max_ready = sem("max_ready")
        exp_ready = sem("exp_ready")
        recip_ready = sem("recip_ready")
        edges_kept = sem("edges_kept")
        pruned_made = sem("pruned_made")
        pruned_stored = sem("pruned_stored")
        row_folded = sem("row_folded")
        node_steps = sem("node_steps")
        mask_staged = sem("mask_staged")
        row_kept = sem("row_kept")
        row_added = sem("row_added")
        msg_kept = sem("msg_kept")
        msg_added = sem("msg_added")
        small_loaded = sem("small_loaded")

        block = ctx.enter_context(nc.Block())

        def half(h):
            return slice(D * h, D * h + D)

        def turned_block(t, b):
            return turned[t][:, CH * b:CH * b + CH]


        def load_rows(sp, src, call, it, first=False):
            for s in range(RING):
                n = it * RING + s
                if not first:
                    sp.wait_ge(rows_used, n + (call * T + 1 - RING))
                    if call is L0:
                        sp.wait_ge(rows_scanned, n + (1 - RING))
                sp.dma_start(ring[s][:, :], src[bass.ds(n * P, P), :]).then_inc(rows_loaded[s], 16)

        def stage_rows(act, call, it, first=False):
            for s in range(RING):
                n = it * RING + s
                if not first:
                    act.wait_ge(rows_used, n + (call * T + 1 - RING))
                act.copy(staged[s][:, :], rows_in[:, bass.ds(n, 1), :]).then_inc(tile_staged, 1)

        def xw_out(b, odd):
            to = (sum_bank if b % 2 == 0 else [nat_bank[1], kept_bank])[odd]
            return to[:, 0:4 * D].rearrange("p (t d) -> p t d", d=D)

        def multiply_rows(pe, call, it, first=False):
            for s in range(RING):
                n = it * RING + s
                pe.wait_ge(rows_loaded[s], (call * (T // RING) + it + 1) * 16)
                pe.wait_ge(tile_staged, n + (call * T + 1))
                for b in range(BANKS):
                    for h in range(2):
                        mm = pe.matmul(bank[b][half(h), :], staged[s][:, :],
                                       ring[s][:, HALF * h + CH * b:HALF * h + CH * b + CH],
                                       start=(first and s == 0), stop=False, skip_group_check=True)
                mm.then_inc(rows_used, 1)

        def clear_sums(pe):
            for b in range(BANKS):
                for h in range(2):
                    mm = pe.matmul(bank[b][half(h), :], zeros[:, 0:D], zeros[:, :],
                                   start=True, stop=False, skip_group_check=True)

        def copy_cols(act, h):
            to = cols_t.rearrange("p (b a c) -> p a b c", a=QUADS, b=BLOCKS)
            for b in range(BANKS):
                first, last = (HALF * h + b * CH) // 32, (HALF * h + (b + 1) * CH) // 32
                for a in range(2 * h, 2 * h + 2):
                    lo, hi = max(first, a * BLOCKS), min(last, (a + 1) * BLOCKS)
                    if lo < hi:
                        at = bank[b][half(h), 32 * (lo - first):32 * (hi - first)]
                        copied = act.copy(to[:, a, lo - a * BLOCKS:hi - a * BLOCKS, :],
                                          at.rearrange("p (b c) -> p b c", c=32))
            copied.then_inc(cols_copied, 1)

        def turn_cols(pe, b, to):
            for j in range(8):
                c0 = P * (8 * b + j)
                mm = pe.transpose(to[:, D * j:D * j + D], cols_t[:, c0:c0 + P], ident[half(0), half(0)])
            mm.then_inc(cols_turned, 1)

        def make_cols_nat(act):
            for a in range(QUADS):
                for j in range(QUADS):
                    made = act.copy(cols_nat[32 * j:32 * j + 32, FLIPS * a:FLIPS * a + FLIPS, :],
                                    cols[32 * a:32 * a + 32, j:BLOCKS:QUADS, :])
            made.then_inc(cols_nat_ready, 1)

        def burst(n):
            return range((n - 1) * FLIP_STEPS // (EARLY - 1), n * FLIP_STEPS // (EARLY - 1)) if n else range(0)

        def flip_blocks(pe, n):
            for i, t in enumerate(burst(n)):
                if n >= 2 and i < len(burst(n - 1)):
                    pe.wait_ge(blocks_copied, burst(n - 1)[i] + 1)
                for j in range(4):
                    c0 = P * (4 * (t % FLIPS) + j)
                    mm = pe.transpose(flip_bank[i][:, P * j:P * j + P], ring[t // FLIPS][:, c0:c0 + P], ident[:, :])
                mm.then_inc(blocks_flipped, 1)

        def copy_flipped(act, n):
            for i, t in enumerate(burst(n)):
                act.wait_ge(blocks_flipped, t + 1)
                if burst(n)[0]:
                    act.wait_ge(flipped_used, burst(n)[0])
                act.copy(flipped[i][:, :], flip_bank[i][:, :]).then_inc(blocks_copied, 1)

        def multiply_flipped(pe, n):
            for i, t in enumerate(burst(n)):
                s = t // FLIPS
                pe.wait_ge(blocks_copied, t + 1)
                for j in range(4):
                    c = 4 * (t % FLIPS) + j
                    mm = pe.matmul(kept_bank[half(j % 2), P * s:P * s + P], cols_nat[:, c, :],
                                   flipped[i][:, P * j:P * j + P], start=(c < 2), stop=(c >= T - 2))
                mm.then_inc(flipped_used, 1)

        class Use:

            def __init__(self, groups, tiles, rounds, first_group=0):
                self.groups, self.tiles, self.rounds, self.first = groups, tiles, rounds, first_group
                self.odd = first_group % 2

        def load_tile(sp, src, slot, g, q, signals, by_rows=False):
            dst = ring[slot][:, :].rearrange("p (R k) -> p R k", R=RSUB)
            width = BPT * 32
            for h, signal in enumerate(signals):
                part = slice(h * RSUB // len(signals), (h + 1) * RSUB // len(signals))
                subs, ks = (part, slice(0, width)) if by_rows else (
                    slice(0, RSUB), slice(h * width // len(signals), (h + 1) * width // len(signals)))
                for a in range(QUADS):
                    c0 = QCOLS * a + q * width
                    piece = src[bass.ds(g * GROUP + 32 * subs.start, 32 * (subs.stop - subs.start)),
                                c0 + ks.start:c0 + ks.stop]
                    sp.dma_start(dst[32 * a:32 * a + 32, subs, ks],
                                 piece.rearrange("(R r) k -> r R k", r=32)).then_inc(signal, 16)

        def load_tiles(sp, src, use, it, units, end=False):
            for u in units:
                sp.wait_ge(halves_turned, (it * (2 * CUTS) + (use.tiles + (u + 1 - RING))) * 2)
                early = [end_loaded[u - units[-2]]] if end and u >= units[-2] else []
                load_tile(sp, src, u % RING, it * 2 + (use.first + u // CUTS), u % CUTS,
                          early + [tiles_loaded[u % RING]], by_rows=(u == units[-1]))

        def tile_views(slot, to):
            return (ring[slot][:, :].rearrange("p (R b c) -> p R b c", R=RSUB, b=BPT),
                    to[:, :].rearrange("p (b R r) -> p R b r", b=BPT, R=RSUB))

        def turn_tile(slot, to, halves=range(2)):
            tile, out = tile_views(slot, to)
            for lo in (BPT // 2 * h for h in halves):
                nc.vector.transpose(out[:, :, lo:lo + BPT // 2, :],
                                    tile[:, :, lo:lo + BPT // 2, :]).then_inc(halves_turned, 1)

        def turn_tiles(dve, use, it, units):
            for u in units:
                dve.wait_ge(tiles_loaded[u % RING], (it * 2 + (use.rounds + (u // RING + 1))) * 64)
                dve.wait_ge(tiles_used, it * (2 * CUTS) + (use.tiles + (u - 1)))
                turn_tile(u % RING, turned[u % 2])

        def multiply_tile(pe, n, k, q, last=CUTS - 1):
            for j in range(BPT):
                if j % (BPT // 2) == 0:
                    pe.wait_ge(halves_turned, n * 2 + (1 if j == 0 else 2))
                mm = pe.matmul(sum_bank[k][half(j % 2), :], cols[:, q * BPT + j, :],
                               turned_block(q % 2, j), start=(q == 0 and j < 2),
                               stop=(q == last and j >= BPT - 2))
            mm.then_inc(tiles_used, 1)

        def close_group(pe, count, k, nat, closing):
            pe.wait_ge(sums_copied, count + 1)
            pe.wait_ge(nat_read, count + 1)
            for t in range(TPG):
                mm = pe.matmul(nat_bank[nat][:, D * t:D * t + D], sums[k][:, P * t:P * t + P],
                               closing, start=True, stop=True)
            mm.then_inc(nat_ready, 1)

        def multiply_tiles(pe, use, it, closing, closed_after, units=range(2 * CUTS)):
            for u in units:
                k, q = (u // CUTS + use.odd) % 2, u % CUTS
                multiply_tile(pe, it * (2 * CUTS) + (use.tiles + u), k, q)
                if q == closed_after:
                    back = 0 if closed_after else 1
                    close_group(pe, it * 2 + (use.groups + u // CUTS - back), (k - back) % 2,
                                (u // CUTS - back) % 2, closing)

        def copy_sums(copy, k, src=None):
            copy(sums[k][:, :], (src or sum_bank[k])[:, :]).then_inc(sums_copied, 1)

        LN_STEPS = 6

        def sum_features(act, src):
            for t in range(TPG):
                last = nc.scalar.activation(ln_c[:, t, :], src[:, t, :], ACT.Copy,
                                            accum_out=ln_sum[:, t:t + 1])
            last.then_inc(ln_sums, 1)

        def sum_squares(act):
            for t in range(TPG):
                last = nc.scalar.activation(ln_y[:, t, :], ln_c[:, t, :], ACT.Square,
                                            accum_out=ln_sum[:, t:t + 1])
            last.then_inc(ln_sums, 1)

        END_K, END_NAT = (KEPT - 1) % 2, (GROUPS - 1) % 2
        end_nat = [nat_bank[END_NAT], flip_bank[0]]

        def turn_end(dve, use):
            tile, out = tile_views(RING - 1, turned[1])
            dve.wait_ge(tiles_used, KEPT * CUTS - 2)
            for t in range(TPG):
                if t == 0:
                    dve.wait_ge(end_loaded[1], 64)
                elif t == 2:
                    dve.wait_ge(tiles_loaded[RING - 1], (use.rounds + 2 * LOOPS) * 64)
                nc.vector.transpose(out[:, 4 * t:4 * t + 4], tile[:, 4 * t:4 * t + 4]
                                    ).then_inc(halves_turned if t % 2 else end_turned, 1)

        def multiply_end(pe):
            for t in range(TPG):
                if t % 2:
                    pe.wait_ge(halves_turned, (KEPT * CUTS - 1) * 2 + t // 2 + 1)
                else:
                    pe.wait_ge(end_turned, t // 2 + 1)
                to, rows = (sum_bank[END_K] if t < 2 else kept_bank), slice(P * t, P * t + P)
                for j in range(BPT):
                    mm = pe.matmul(to[half(j % 2), rows], cols[:, BLOCKS - BPT + j, :], turned_block(1, j)[:, rows],
                                   start=(t >= 2 and j < 2), stop=(j >= BPT - 2), skip_group_check=True)
                if t % 2:
                    mm.then_inc(end_multiplied if t == 1 else tiles_used, 1)

        def sum_end(dve):
            dve.wait_ge(end_multiplied, 1)
            nc.vector.tensor_copy(sums[END_K][:, :], sum_bank[END_K][:, :]).then_inc(end_copied, 1)
            dve.wait_ge(tiles_used, KEPT * CUTS)
            dve.wait_ge(end_copied, 1)
            late = slice(2 * P, TPG * P)
            nc.vector.tensor_tensor(sums[END_K][:, late], sums[END_K][:, late], kept_bank[:, late],
                                    ALU.add).then_inc(sums_copied, 1)

        def close_end(pe, closing):
            for h in range(2):
                if h == 0:
                    pe.wait_ge(end_copied, 1)
                    pe.wait_ge(nat_read, GROUPS)
                else:
                    pe.wait_ge(sums_copied, GROUPS)
                for t in range(2):
                    rows = slice(P * (2 * h + t), P * (2 * h + t) + P)
                    mm = pe.matmul(end_nat[h][:, D * t:D * t + D], sums[END_K][:, rows], closing,
                                   start=True, stop=True)
                mm.then_inc(end_closed if h == 0 else nat_ready, 1)

        def store_group(eng, g, src, signal):
            eng.dma_start(out.rearrange("(g t p) d -> g p t d", p=P, t=TPG)[bass.ds(g, 1)].squeeze(0),
                          src[:, :, :]).then_inc(signal, 16)

        def spread(ap):
            return ap.unsqueeze(2).to_broadcast([P, TPG, D])

        def over_tiles(ap):
            return ap.unsqueeze(1).to_broadcast([P, TPG, D])

        L0 = 0
        END_VAR = [3, 9, 14]
        END_STEPS = 16
        LOOPED = RING + 1
        LOOPS = (KEPT - LOOPED) // 2
        NORMED = GROUPS - 1
        SUMS0, STEPS0 = 6, 3 * LN_STEPS + 4
        SUMS1, STEPS1 = 2, LN_STEPS

        class Steps:

            def __init__(self, pool, base):
                self.pool, self.base, self.done = pool, base, 0

            def wait(self):
                self.done += 1
                self.pool.wait_ge(ln_steps, self.base + self.done)

            def __call__(self, out, a, b, op):
                nc.gpsimd.tensor_tensor(out, a, b, op).then_inc(ln_steps, 1)
                self.wait()

        def layer_norm(pool, step, src, sums_base, dst, after_mean=None, stored=None):
            pool.wait_ge(ln_sums, sums_base + 1)
            nc.gpsimd.tensor_tensor(ln_mean[:, :], ln_sum[:, :], neg_inv_d[:, :], ALU.mult).then_inc(ln_steps, 1)
            if after_mean:
                after_mean()
            step.wait()
            step(ln_c[:, :, :], src[:, :, :], spread(ln_mean[:, :]), ALU.add)
            pool.wait_ge(ln_sums, sums_base + 2)
            step(ln_var[:, :], ln_sum[:, :], inv_d[:, :], ALU.mult)
            step(ln_var[:, :], ln_var[:, :], eps_tile[:, :], ALU.add)
            step(ln_rstd[:, :], ln_var[:, :], minus_half[:, :], ALU.pow)
            if stored is not None:
                pool.wait_ge(ln_stored, stored)
            step(dst[:, :, :], ln_c[:, :, :], spread(ln_rstd[:, :]), ALU.mult)

        def edges_may_survive(eng):
            eng.wait_ge(flag_made, 1)
            return eng.value_load(flag[0:1, 0:1], min_val=0, max_val=1)

        STAGES = 9
        PROJECT, EDGES, ATTEND, COMPRESS, TURN_XN, PRUNE, NODES, GATHER, SCATTER = range(STAGES)
        SHARERS = 4
        CHUNKS = N // CH

        def meet(eng, l, stage):
            eng.drain().then_inc(gate, 1)
            eng.wait_ge(gate, (l * STAGES + (stage + 1)) * SHARERS)
            eng.sem_inc(passed, 1)


        def layer1_use(l):
            return Use((l + 1) * GROUPS, (l * GROUPS + KEPT) * CUTS, l * GROUPS + (1 + KEPT - LOOPED))

        def sp_score_rows(sp, l, k):
            with sp.Fori(0, T) as i:
                n = (l * 2 + k) * T + i
                sp.dma_start(h_rows[:, :], adj[bass.ds(i * P, P), :]).then_inc(h_loaded, 16)
                if k == 1:
                    sp.wait_ge(pruned_made, l * T + i + 1)
                    sp.dma_start(pruned[bass.ds(i * P, P), :], logits[:, :]).then_inc(pruned_stored, 16)
                sp.wait_ge(row_folded, n + 1)
                sp.sem_inc(passed, 1)

        def message_sp(sp):
            for dst, src in ((w_qv_sb[:, :], w_qv), (w_q_sb[:, :], w_q), (theta2[half(0), :], theta),
                             (theta2[half(1), :], theta), (b_q_sb[:, :], b_q),
                             (b_v_sb[:, :], b_v.partition_broadcast(P))):
                sp.dma_start(dst, src).then_inc(weights_loaded, 16)
            sp.wait_ge(weights_loaded, 16 * 6)
            with sp.Fori(0, ROUNDS) as l:
                meet(sp, l, PROJECT)
                meet(sp, l, EDGES)
                with sp.Fori(0, T // RING) as it:
                    load_rows(sp, adj, l * 2 + 1, it)
                meet(sp, l, ATTEND)
                sp_score_rows(sp, l, 0)
                meet(sp, l, COMPRESS)
                meet(sp, l, TURN_XN)
                meet(sp, l, PRUNE)
                sp_score_rows(sp, l, 1)
                sp.wait_ge(pruned_stored, (l + 1) * T * 16)
                sp.sem_inc(passed, 1)
                meet(sp, l, NODES)
                meet(sp, l, GATHER)
                with sp.Fori(0, T // RING) as it:
                    load_rows(sp, pruned, l * 2 + 2, it)
                meet(sp, l, SCATTER)
                with sp.Fori(0, GROUPS // 2) as it:
                    load_tiles(sp, pruned, layer1_use(l), it,
                               range(2 * CUTS))
            meet(sp, ROUNDS, PROJECT)

        def pe_score_rows(pe, l, k):
            moving = edge_t if k == 0 else xt_all
            with pe.Fori(0, T) as i:
                n = (l * 2 + k) * T + i
                pe.wait_ge(row_staged, n + 1)
                for c in range(CHUNKS):
                    if c >= 4:
                        pe.wait_ge(chunk_masked, n * CHUNKS + (c - 3))
                    pe.matmul(bank[c % 4][:, :], xt_tile[:, :], moving[:, CH * c:CH * c + CH],
                              start=True, stop=True).then_inc(chunk_scored, 1)
                if k == 0:
                    pe.wait_ge(recip_ready, n + 1)
                    for j in range(T):
                        mm = pe.matmul(bank[4][:, j:j + 1], logits[:, P * j:P * j + P], recip[:, :],
                                       start=True, stop=True)
                else:
                    pe.wait_ge(pruned_made, l * T + i + 1)
                    for b in range(BLOCKS):
                        for a in range(QUADS):
                            c0 = QCOLS * a + 32 * b
                            mm = pe.matmul(bank[4][32 * a:32 * a + 32, b:b + 1], logits[:, c0:c0 + 32],
                                           ones[:, 0:1], start=True, stop=True)
                mm.then_inc(row_folded, 1)

        def act_score_rows(act, l, k):
            with act.Fori(0, T) as i:
                n = (l * 2 + k) * T + i
                act.wait_ge(max_ready, n + 1)
                nc.scalar.activation(logits[:, :], logits[:, :], ACT.Exp, bias=neg_max[:, :],
                                     accum_out=part_sum[:, :]).then_inc(exp_ready, 1)

        def dve_score_rows(dve, l, k):
            with dve.Fori(0, T) as i:
                n = (l * 2 + k) * T + i
                nc.vector.tensor_copy(xt_tile[:, :], xt_all[:, bass.ds(i * P, P)]).then_inc(row_staged, 1)
                dve.wait_ge(h_loaded, (n + 1) * 16)
                for c in range(CHUNKS):
                    cs = slice(CH * c, CH * c + CH)
                    dve.wait_ge(chunk_scored, n * CHUNKS + (c + 1))
                    nc.vector.scalar_tensor_tensor(logits[:, cs], bank[c % 4][:, :], SCALE if k == 0 else 1.0,
                                                   h_rows[:, cs], ALU.mult, ALU.mult).then_inc(chunk_masked, 1)
                dve.wait_ge(chunk_masked, (n + 1) * CHUNKS)
                nc.vector.tensor_reduce(neg_max[:, :], logits[:, :], X, ALU.max, negate=True).then_inc(max_ready, 1)
                dve.wait_ge(exp_ready, n + 1)
                nc.vector.reciprocal(recip[:, :], part_sum[:, :]).then_inc(recip_ready, 1)
                if k == 0:
                    dve.wait_ge(row_folded, n + 1)
                    nc.vector.tensor_tensor(att[:, :], att[:, :], bank[4][:, 0:T], ALU.add).then_inc(edges_kept, 1)
                else:
                    dve.wait_ge(recip_ready, n + 1)
                    nc.vector.tensor_scalar(logits[:, :], logits[:, :], recip[:, :], threshold[:, :],
                                            ALU.mult, ALU.is_ge).then_inc(edges_kept, 1)
                    nc.vector.tensor_copy(mask_tile[:, :], comp_mask[:, bass.ds(i, 1)]).then_inc(mask_staged, 1)
                    dve.wait_ge(edges_kept, n + 1)
                    dve.wait_ge(mask_staged, l * T + i + 1)
                    nc.vector.scalar_tensor_tensor(logits[:, :], logits[:, :], mask_tile[:, :], h_rows[:, :],
                                                   ALU.mult, ALU.mult,
                                                   accum_out=conn_tile[:, :]).then_inc(pruned_made, 1)
                    dve.wait_ge(pruned_made, l * T + i + 1)
                    nc.vector.tensor_copy(conn[:, bass.ds(i, 1)], conn_tile[:, :])
                    dve.wait_ge(row_folded, n + 1)
                    nc.vector.tensor_tensor(edge_deg[:, :], edge_deg[:, :], bank[4][:, 0:BLOCKS],
                                            ALU.add).then_inc(row_added, 1)
                    dve.wait_ge(pruned_stored, (l * T + i + 1) * 16)
                    dve.wait_ge(row_added, l * T + i + 1)

        def node_chain(engine, l, stage):
            count, before = [0], 0 if stage == COMPRESS else COMPRESS_STEPS

            def step(who, make):
                if who is engine:
                    if count[0]:
                        engine.wait_ge(node_steps, l * (COMPRESS_STEPS + NODES_STEPS) + (before + count[0]))
                    make().then_inc(node_steps, 1)
                count[0] += 1

            v, a, p = nc.vector, nc.scalar, nc.tensor

            def tiles_of(ap):
                return ap.unsqueeze(2).to_broadcast([P, T, D])

            def sum_squares_of(src, dst):
                step(v, lambda: v.tensor_tensor(tmp, src, src, ALU.mult))
                step(v, lambda: v.tensor_reduce(dst, tmp, X, ALU.add))
                step(v, lambda: v.tensor_scalar(dst, dst, 1e-16, None, ALU.max))

            def softmax_mask(z, e, mask):
                step(v, lambda: v.tensor_reduce(part[:, :], z, X, ALU.max))
                step(v, lambda: v.tensor_scalar(diagonal[:, :], ident[:, :], part[:, :], None, ALU.mult))
                step(p, lambda: p.matmul(bank[0][:, 0:P], ones[:, :], diagonal[:, :], start=True, stop=True))
                step(v, lambda: v.tensor_reduce(neg_max[:, :], bank[0][:, 0:P], X, ALU.max, negate=True))
                step(a, lambda: a.activation(e, z, ACT.Exp, bias=neg_max[:, :], accum_out=part_sum[:, :]))
                step(p, lambda: p.matmul(bank[1][:, 0:1], ones[:, :], part_sum[:, :], start=True, stop=True))
                step(v, lambda: v.reciprocal(recip[:, :], bank[1][:, 0:1]))
                step(v, lambda: v.tensor_scalar(mask, e, recip[:, :], threshold[:, :], ALU.mult, ALU.is_ge))

            if stage == COMPRESS:
                sum_squares_of(xw_all[:, :, :], node_a[:, :])
                step(a, lambda: a.activation(node_b[:, :], node_a[:, :], ACT.Sqrt))
                step(v, lambda: v.tensor_scalar(att[:, :], att[:, :], 0.5 / N, None, ALU.mult))
                step(v, lambda: v.scalar_tensor_tensor(node_a[:, :], node_b[:, :], 0.5, att[:, :],
                                                       ALU.mult, ALU.add))
                softmax_mask(node_a[:, :], node_b[:, :], comp_mask[:, :])
                step(v, lambda: v.tensor_tensor(x_cur[:, :, :], x_cur[:, :, :], tiles_of(comp_mask[:, :]), ALU.mult))
                sum_squares_of(x_cur[:, :, :], node_a[:, :])
                step(a, lambda: a.activation(feat_mag[:, :], node_a[:, :], ACT.Sqrt))
                step(v, lambda: v.tensor_scalar(node_a[:, :], feat_mag[:, :], 1e-8, None, ALU.max))
                step(v, lambda: v.reciprocal(node_b[:, :], node_a[:, :]))
                step(v, lambda: v.tensor_tensor(rows_in[:, :, :], x_cur[:, :, :], tiles_of(node_b[:, :]), ALU.mult))
            else:
                step(v, lambda: v.tensor_tensor(node_a[:, :], conn[:, :], feat_mag[:, :], ALU.mult))
                softmax_mask(node_a[:, :], node_b[:, :], node_c[:, :])
                step(v, lambda: v.tensor_scalar(node_a[:, :], conn[:, :], 0.0, None, ALU.is_gt))
                step(v, lambda: v.tensor_tensor(node_c[:, :], node_c[:, :], node_a[:, :], ALU.mult))
                step(v, lambda: v.tensor_tensor(node_c[:, :], node_c[:, :], comp_mask[:, :], ALU.mult))
                step(v, lambda: v.tensor_scalar(node_a[:, :], conn[:, :], DEG_EPS, None, ALU.max))
                step(a, lambda: a.activation(node_b[:, :], node_a[:, :], ACT.Sqrt))
                step(v, lambda: v.reciprocal(dv[:, :], node_b[:, :]))
                step(v, lambda: v.tensor_tensor(node_c[:, :], node_c[:, :], dv[:, :], ALU.mult))
                step(v, lambda: v.tensor_tensor(rows_in[:, :, :], xw_all[:, :, :], tiles_of(node_c[:, :]), ALU.mult))
                step(v, lambda: v.tensor_scalar(edge_deg[:, :], edge_deg[:, :], DEG_EPS, None, ALU.max))
                step(v, lambda: v.reciprocal(node_a[:, :], edge_deg[:, :]))
            assert count[0] == (COMPRESS_STEPS if stage == COMPRESS else NODES_STEPS)

        COMPRESS_STEPS, NODES_STEPS = 22, 19

        def pe_turn_x(pe, l, k):
            with pe.Fori(0, T) as i:
                n = (l * 2 + k) * T + i
                pe.wait_ge(x_staged, n + 1)
                pe.transpose(bank[0][:, 0:P], x_pad[:, :], ident[:, :]).then_inc(x_turned, 1)
                if k == 0:
                    pe.wait_ge(xt_ready, n + 1)
                    pe.matmul(bank[1][:, 0:2 * D], xt_tile[:, :], w_qv_sb[:, :], start=True, stop=True)
                    pe.matmul(bank[2][0:D, 0:P], w_q_sb[:, :], xt_tile[:, :],
                              start=True, stop=True).then_inc(projected, 1)

        def message_pe(pe):
            with pe.Fori(0, ROUNDS) as l:
                meet(pe, l, PROJECT)
                pe_turn_x(pe, l, 0)
                meet(pe, l, EDGES)
                clear_sums(pe)
                with pe.Fori(0, T // RING) as it:
                    multiply_rows(pe, l * 2 + 1, it)
                meet(pe, l, ATTEND)
                pe_score_rows(pe, l, 0)
                meet(pe, l, COMPRESS)
                node_chain(pe, l, COMPRESS)
                meet(pe, l, TURN_XN)
                pe_turn_x(pe, l, 1)
                meet(pe, l, PRUNE)
                pe_score_rows(pe, l, 1)
                meet(pe, l, NODES)
                node_chain(pe, l, NODES)
                meet(pe, l, GATHER)
                clear_sums(pe)
                with pe.Fori(0, T // RING) as it:
                    multiply_rows(pe, l * 2 + 2, it)
                pe.wait_ge(cols_copied, l * 2 + 4)
                pe.sem_inc(passed, 1)
                for b in range(BANKS):
                    turn_cols(pe, b, bank[b])
                meet(pe, l, SCATTER)
                with pe.Fori(0, GROUPS // 2) as it:
                    multiply_tiles(pe, layer1_use(l), it, theta2, CUTS - 1)
            meet(pe, ROUNDS, PROJECT)

        def act_turn_x(act, l, k):
            with act.Fori(0, T) as i:
                n = (l * 2 + k) * T + i
                act.wait_ge(x_turned, n + 1)
                if k == 0:
                    act.copy(xt_tile[:, :], bank[0][0:D, 0:P]).then_inc(xt_ready, 1)
                    act.wait_ge(projected, l * T + i + 1)
                    nc.scalar.activation(xt_all[:, bass.ds(i * P, P)], bank[2][0:D, 0:P], ACT.Identity,
                                         bias=b_q_sb[:, :]).then_inc(q_kept, 1)
                else:
                    act.copy(xt_all[:, bass.ds(i * P, P)], bank[0][0:D, 0:P]).then_inc(xt_ready, 1)

        def message_act(act):
            with act.Fori(0, ROUNDS) as l:
                meet(act, l, PROJECT)
                act_turn_x(act, l, 0)
                meet(act, l, EDGES)
                with act.Fori(0, T // RING) as it:
                    stage_rows(act, l * 2 + 1, it)
                act.wait_ge(rows_used, (l * 2 + 2) * T)
                for b in range(BANKS):
                    for h in range(2):
                        c0 = HALF * h + CH * b
                        act.copy(edge_t[:, c0:c0 + CH], bank[b][half(h), :])
                meet(act, l, ATTEND)
                act_score_rows(act, l, 0)
                meet(act, l, COMPRESS)
                node_chain(act, l, COMPRESS)
                meet(act, l, TURN_XN)
                act_turn_x(act, l, 1)
                meet(act, l, PRUNE)
                act_score_rows(act, l, 1)
                meet(act, l, NODES)
                node_chain(act, l, NODES)
                meet(act, l, GATHER)
                with act.Fori(0, T // RING) as it:
                    stage_rows(act, l * 2 + 2, it)
                act.wait_ge(rows_used, (l * 2 + 3) * T)
                for h in range(2):
                    copy_cols(act, h)
                meet(act, l, SCATTER)
                with act.Fori(0, GROUPS // 2) as it:
                    for k in range(2):
                        act.wait_ge(tiles_used, (it * 2 + (l * GROUPS + (KEPT + k + 1))) * CUTS)
                        copy_sums(act.copy, k)
            meet(act, ROUNDS, PROJECT)
            act.wait_ge(msg_added, 1)
            with act.Fori(0, GROUPS) as g:
                p0 = g * STEPS1 + NORMED * STEPS0
                for t in range(TPG):
                    last = nc.scalar.activation(ln_h[:, t, :], x_cur[:, bass.ds(g * TPG + t, 1), :].squeeze(1),
                                                ACT.Copy, accum_out=ln_sum[:, t:t + 1])
                last.then_inc(ln_sums, 1)
                act.wait_ge(ln_steps, p0 + 2)
                sum_squares(act)
                act.wait_ge(ln_steps, p0 + STEPS1)
                store_group(act, g, ln_out, ln_stored)
            act.wait_ge(ln_stored, 16 * (NORMED + GROUPS + 1))

        def dve_turn_x(dve, l, k):
            src = x_cur if k == 0 else rows_in
            with dve.Fori(0, T) as i:
                n = (l * 2 + k) * T + i
                nc.vector.tensor_copy(x_pad[:, 0:D], src[:, bass.ds(i, 1), :].squeeze(1)).then_inc(x_staged, 1)
                if k == 0:
                    m = l * T + i + 1
                    dve.wait_ge(projected, m)
                    nc.vector.tensor_copy(xw_all[:, bass.ds(i, 1), :].squeeze(1), bank[1][:, 0:D])
                    nc.vector.tensor_tensor(rows_in[:, bass.ds(i, 1), :].squeeze(1), bank[1][:, D:2 * D],
                                            b_v_sb[:, :], ALU.add).then_inc(row_kept, 1)
                    dve.wait_ge(q_kept, m)
                    dve.wait_ge(row_kept, m)
                else:
                    dve.wait_ge(xt_ready, n + 1)

        def message_dve(dve):
            dve.wait_ge(ln_stored, 16 * (NORMED + 1))
            for h in range(2):
                dve.wait_ge(end_steps[h], END_STEPS)
            nc.vector.tensor_copy(x_cur[:, :, :], x_all[:, :, :])
            nc.vector.memset(ones[:, :], 1.0)
            nc.vector.memset(x_pad[:, :], 0.0)
            for r in range(ROUNDS):
                nc.vector.memset(thresholds[:, r:r + 1], THETA[r])
            with dve.Fori(0, ROUNDS) as l:
                meet(dve, l, PROJECT)
                nc.vector.tensor_copy(threshold[:, :], thresholds[:, bass.ds(l, 1)])
                nc.vector.memset(att[:, :], 0.0)
                nc.vector.memset(edge_deg[:, :], 0.0)
                dve_turn_x(dve, l, 0)
                nc.vector.memset(zeros[:, :], 0.0)
                meet(dve, l, EDGES)
                meet(dve, l, ATTEND)
                dve_score_rows(dve, l, 0)
                meet(dve, l, COMPRESS)
                node_chain(dve, l, COMPRESS)
                meet(dve, l, TURN_XN)
                dve_turn_x(dve, l, 1)
                meet(dve, l, PRUNE)
                dve_score_rows(dve, l, 1)
                meet(dve, l, NODES)
                node_chain(dve, l, NODES)
                nc.vector.memset(zeros[:, :], 0.0)
                meet(dve, l, GATHER)
                for b in range(BANKS):
                    dve.wait_ge(cols_turned, (l + 1) * BANKS + (b + 1))
                    nc.vector.tensor_tensor(cols[:, 8 * b:8 * b + 8, :],
                                            bank[b][:, :].rearrange("p (t d) -> p t d", d=D),
                                            node_a[:, 8 * b:8 * b + 8].unsqueeze(2).to_broadcast([P, 8, D]), ALU.mult)
                meet(dve, l, SCATTER)
                with dve.Fori(0, GROUPS // 2) as it:
                    for k in range(2):
                        turn_tiles(dve, layer1_use(l), it,
                                   range(k * CUTS, k * CUTS + CUTS))
                        g = it * 2 + k
                        dve.wait_ge(nat_ready, g + (l * GROUPS + (GROUPS + 1)))
                        nc.vector.tensor_tensor(ln_c[:, :, :], nat_bank[k][:, 0:TPG * D].rearrange("p (t d) -> p t d", d=D),
                                                dv[:, bass.ds(g * TPG, TPG)].unsqueeze(2).to_broadcast([P, TPG, D]),
                                                ALU.mult).then_inc(nat_read, 1)
                        dve.wait_ge(nat_read, g + (l * GROUPS + (GROUPS + 3)))
                        nc.vector.tensor_scalar(x_cur[:, bass.ds(g * TPG, TPG), :], ln_c[:, :, :], 0.0, None,
                                                ALU.max).then_inc(msg_kept, 1)
                        dve.wait_ge(msg_kept, g + (l * GROUPS + 1))
            meet(dve, ROUNDS, PROJECT)
            nc.vector.tensor_tensor(x_cur[:, :, :], x_cur[:, :, :], x_all[:, :, :], ALU.add).then_inc(msg_added, 1)

        def message_pool(pool):
            pool.wait_ge(gate, (ROUNDS * STAGES + 1) * SHARERS)
            with pool.Fori(0, GROUPS) as g:
                step = Steps(pool, g * STEPS1 + NORMED * STEPS0)
                layer_norm(pool, step, ln_h, g * SUMS1 + NORMED * SUMS0, ln_out,
                           stored=(g + (NORMED + 1)) * 16)

        loop_use = Use(LOOPED + 1, LOOPED * CUTS, 1, LOOPED)

        @block.sync
        def _(sp):
            sp.dma_start(x_all[:, :, :], x.rearrange("(t p) d -> p t d", p=P)).then_inc(x_loaded, 16)
            for h in range(2):
                sp.dma_start(w_ui_sb[half(h), :], w_ui).then_inc(const_loaded, 16)
            sp.dma_start(diag_sb[:, :], diag).then_inc(const_loaded, 16)
            sp.dma_start(par_sb[:, :], par.partition_broadcast(P)).then_inc(const_loaded, 16)
            load_rows(sp, adj, L0, 0, first=True)
            with sp.Fori(1, T // RING) as it:
                load_rows(sp, adj, L0, it)
            def load_spare(g, q, turned_before):
                if turned_before is not None:
                    sp.wait_ge(halves_turned, turned_before * 2)
                load_tile(sp, adj, RING + q % SPARE, g, q, [spare_loaded[q % SPARE]])

            for q in range(CUTS):
                load_spare(0, q, q - SPARE + 1 if q >= SPARE else None)
            with sp.Fori(1, RING) as g:
                for q in range(CUTS):
                    load_spare(g, q, g * CUTS + (q - SPARE + 1))
            sp.wait_ge(rows_scanned, T)
            for u in range(RING):
                sp.wait_ge(blocks_flipped, (u + 1) * FLIPS)
                load_tile(sp, adj, u, RING, u, [tiles_loaded[u]])
            with sp.Fori(0, LOOPS - 1) as it:
                load_tiles(sp, adj, loop_use, it, range(2 * CUTS))
            load_tiles(sp, adj, loop_use, LOOPS - 1, range(2 * CUTS), end=True)
            for h in range(2):
                both = slice(2 * h, 2 * h + 2)
                sp.wait_ge(end_steps[h], END_STEPS)
                sp.dma_start(out.rearrange("(g t p) d -> g p t d", p=P, t=TPG)[KEPT - 1][:, both],
                             end_y[:, both, :]).then_inc(end_stored, 16)
            sp.wait_ge(end_stored, 16 * 2)
            with sp.If(edges_may_survive(sp) > 0):
                message_sp(sp)

        @block.gpsimd
        def _(pool):
            nc.gpsimd.memset(ident[:, :], 0.0).then_inc(ident_clear, 1)
            nc.gpsimd.memset(stack[:, :], 0.0).then_inc(ident_clear, 1)
            for tile, value in ((minus_half, -0.5), (inv_d, 1.0 / D), (neg_inv_d, -1.0 / D), (eps_tile, LN_EPS)):
                nc.gpsimd.memset(tile[:, :], value).then_inc(ident_clear, 1)
            pool.wait_ge(ident_clear, 6)
            nc.gpsimd.affine_select(out=ident[:, :], in_=ident[:, :], compare_op=ALU.not_equal, fill=1.0,
                                    base=0, pattern=[[-1, P]], channel_multiplier=1).then_inc(const_made, 1)
            for h in range(2):
                pool.wait_ge(const_made, 1 + h)
                nc.gpsimd.affine_select(out=stack[:, :], in_=stack[:, :], compare_op=ALU.not_equal, fill=1.0,
                                        base=-D * h, pattern=[[-1, D]],
                                        channel_multiplier=1).then_inc(const_made, 1)
            pool.wait_ge(max_found, 1)
            nc.gpsimd.partition_all_reduce(all_max[:, :], part_max[:, :], P, bass.bass_isa.ReduceOp.max).then_inc(max_found, 1)
            pool.wait_ge(max_found, 2)
            nc.gpsimd.tensor_scalar(flag[:, :], all_max[:, :], LIMIT, None, ALU.is_ge).then_inc(flag_made, 1)

            pool.sem_inc(ln_stored, 16)
            pool.wait_ge(small_loaded, 16 * 2)
            def finish_group(count, tiles):
                s0 = count * SUMS0
                step = Steps(pool, count * STEPS0)
                layer_norm(pool, step, ln_h, s0, ln_y,
                           after_mean=lambda: nc.gpsimd.tensor_copy(ln_x[:, :, :], x_all[:, tiles, :]))
                step(ln_y[:, :, :], ln_y[:, :, :], over_tiles(gamma_sb[:, :]), ALU.mult)
                step(ln_y[:, :, :], ln_y[:, :, :], over_tiles(beta_sb[:, :]), ALU.add)
                step(ln_y[:, :, :], ln_y[:, :, :], ln_x[:, :, :], ALU.add)
                step(ln_h[:, :, :], ln_y[:, :, :], ln_x[:, :, :], ALU.add)
                layer_norm(pool, step, ln_h, s0 + 2, ln_y)
                layer_norm(pool, step, ln_y, s0 + 4, ln_out, stored=(count + 1) * 16,
                           after_mean=lambda: nc.gpsimd.tensor_copy(x_all[:, tiles, :], ln_y[:, :, :]))

            with pool.Fori(0, RING) as m:
                finish_group(m, bass.ds(m * TPG, TPG))
            finish_group(RING, slice(KEPT * TPG, T))
            tiles = slice((KEPT - 1) * TPG, KEPT * TPG)
            nc.gpsimd.tensor_tensor(end_add[:, :, :], x_all[:, tiles, :], over_tiles(beta_sb[:, :]),
                                    ALU.add).then_inc(add_made, 1)
            pool.wait_ge(add_made, 1)
            nc.gpsimd.tensor_tensor(end_add[:, :, :], end_add[:, :, :], x_all[:, tiles, :],
                                    ALU.add).then_inc(add_made, 1)
            with pool.Fori(RING + 1, NORMED) as m:
                finish_group(m, bass.ds((m - 1) * TPG, TPG))
            for n in range(3):
                for h in range(2):
                    both = slice(2 * h, 2 * h + 2)
                    pool.wait_ge(end_steps[h], END_VAR[n])
                    nc.gpsimd.tensor_tensor(end_rstd[:, both], end_var[:, both], minus_half[:, both],
                                            ALU.pow).then_inc(end_steps[h], 1)
            with pool.If(edges_may_survive(pool) > 0):
                message_pool(pool)

        @block.scalar
        def _(act):
            act.dma_start(gamma_sb[:, :], gamma.partition_broadcast(P)).then_inc(small_loaded, 16)
            act.dma_start(beta_sb[:, :], beta.partition_broadcast(P)).then_inc(small_loaded, 16)
            for b in range(BANKS):
                act.wait_ge(pairs_turned, b + 1)
                act.copy(xt_pairs[:, CH * b:CH * b + CH], bank[b % 4][:, :]).then_inc(pairs_copied, 1)
            act.wait_ge(e_made, 1)
            stage_rows(act, L0, 0, first=True)
            act.wait_ge(e_made, BANKS)
            with act.Fori(1, T // RING) as it:
                stage_rows(act, L0, it)
            act.wait_ge(rows_used, T)
            copy_cols(act, 0)
            copy_cols(act, 1)
            for b in range(BANKS):
                act.wait_ge(cols_turned, b + 1)
                act.copy(cols[:, 8 * b:8 * b + 8, :],
                         bank[b][:, :].rearrange("p (t d) -> p t d", d=D)).then_inc(cols_made, 1)
            act.wait_ge(cols_made, BANKS)
            make_cols_nat(act)

            def sum_part(count, g, part, nat):
                p0, s0 = count * STEPS0, count * SUMS0
                if part == 0:
                    act.wait_ge(nat_ready, count + 1)
                    for t in range(TPG):
                        last = nc.scalar.activation(ln_h[:, t, :], nat_bank[nat][:, D * t:D * t + D], ACT.Copy,
                                                    accum_out=ln_sum[:, t:t + 1])
                    last.then_inc(ln_sums, 1)
                    act.wait_ge(ln_sums, s0 + 1)
                    act.sem_inc(nat_read, 1)
                    act.wait_ge(ln_steps, p0 + 2)
                    sum_squares(act)
                elif part < 3:
                    act.wait_ge(ln_steps, p0 + (LN_STEPS + 4 if part == 1 else 2 * LN_STEPS + 4))
                    sum_features(act, ln_h if part == 1 else ln_y)
                    act.wait_ge(ln_steps, p0 + (LN_STEPS + 6 if part == 1 else 2 * LN_STEPS + 6))
                    sum_squares(act)
                else:
                    act.wait_ge(ln_steps, p0 + STEPS0)
                    store_group(act, g, ln_out, ln_stored)

            for n in range(EARLY):
                copy_flipped(act, n)
                g, q = n // CUTS, n % CUTS
                if q and g >= 1:
                    sum_part(g - 1, g - 1, q - 1, (g - 1) % 2)
                elif q == 0 and g >= 2:
                    sum_part(g - 2, g - 2, 3, g % 2)
            sum_part(RING - 2, RING - 2, 3, 0)
            for part in range(4):
                sum_part(RING - 1, RING - 1, part, 1)
            for part in range(4):
                sum_part(RING, KEPT, part, 0)
            with act.Fori(0, (NORMED - RING - 1) // 2) as it:
                for k in range(2):
                    for part in range(4):
                        sum_part(it * 2 + (RING + 1 + k), it * 2 + (RING + k), part, (RING + 1 + k) % 2)
            act.wait_ge(ln_stored, 16 * (NORMED + 1))
            with act.If(edges_may_survive(act) > 0):
                message_act(act)

        @block.vector
        def _(dve):
            dve.wait_ge(const_loaded, 16 * 4)
            nc.vector.tensor_tensor(pp[:, :], par_sb[:, 0:4:2], par_sb[:, 1:4:2], ALU.mult).then_inc(pp_made, 1)
            dve.wait_ge(pp_made, 1)
            for k, (a, b) in enumerate(((0, USER_TILES), (USER_TILES, T))):
                nc.vector.tensor_scalar(diag_sb[:, a:b], diag_sb[:, a:b], pp[:, k:k + 1], None,
                                        ALU.mult).then_inc(pp_made, 1)
            dve.wait_ge(pp_made, 3)
            dve.wait_ge(x_loaded, 16)
            for b in range(BANKS):
                dve.wait_ge(xw_done, b + 1)
                for odd in range(2):
                    tiles = slice(8 * b + odd, 8 * b + 8, 2)
                    scaled = nc.vector.tensor_tensor(rows_in[:, tiles, :], xw_out(b, odd),
                                                     diag_sb[:, tiles].unsqueeze(2).to_broadcast([P, 4, D]), ALU.mult)
                scaled.then_inc(e_scaled, 1)
                dve.wait_ge(e_scaled, b + 1)
                t8 = slice(8 * b, 8 * b + 8)
                nc.vector.tensor_tensor(rows_in[:, t8, :], rows_in[:, t8, :], x_all[:, t8, :],
                                        ALU.add).then_inc(e_made, 1)
            with dve.Fori(0, T // RING) as it:
                for s in range(RING):
                    dve.wait_ge(rows_loaded[s], (it + 1) * 16)
                    nc.vector.tensor_reduce(row_max[:, bass.ds(it * RING + s, 1)], ring[s][:, :], X, ALU.max,
                                            apply_absolute_value=True).then_inc(rows_scanned, 1)
            dve.wait_ge(rows_scanned, T)
            nc.vector.tensor_reduce(part_max[:, :], row_max[:, :], X, ALU.max).then_inc(max_found, 1)
            def turn_spare(n, q):
                dve.wait_ge(spare_loaded[q % SPARE], (n // SPARE + 1) * 64)
                turn_tile(RING + q % SPARE, turned[q % 2])

            turn_spare(0, 0)
            dve.wait_ge(cols_turned, BANKS)
            turn_spare(1, 1)
            for q in range(2, CUTS):
                dve.wait_ge(tiles_used, q - 1)
                turn_spare(q, q)
            for g in range(1, RING):
                for q in range(CUTS):
                    n = g * CUTS + q
                    dve.wait_ge(tiles_used, n - 1)
                    turn_spare(n, q)
                    if q == 0:
                        dve.wait_ge(tiles_used, n)
                        copy_sums(nc.vector.tensor_copy, (g - 1) % 2)
            for q in range(CUTS):
                n = EARLY + q
                dve.wait_ge(tiles_loaded[q], 64)
                dve.wait_ge(tiles_used, n - 1)
                turn_tile(q, turned[q % 2])
                if q == 0:
                    dve.wait_ge(tiles_used, EARLY)
                    copy_sums(nc.vector.tensor_copy, 1)
                elif q == 1:
                    dve.wait_ge(flipped_used, FLIP_STEPS)
                    copy_sums(nc.vector.tensor_copy, 0, kept_bank)

            def turn_group(it, k):
                turn_tiles(dve, loop_use, it, range(k * CUTS, k * CUTS + 1))
                dve.wait_ge(tiles_used, it * (2 * CUTS) + (LOOPED + k) * CUTS)
                copy_sums(nc.vector.tensor_copy, (LOOPED - 1 + k) % 2)
                turn_tiles(dve, loop_use, it, range(k * CUTS + 1, k * CUTS + CUTS))

            with dve.Fori(0, LOOPS - 1) as it:
                for k in range(2):
                    turn_group(it, k)
            turn_group(LOOPS - 1, 0)
            dve.wait_ge(tiles_used, (KEPT - 1) * CUTS)
            copy_sums(nc.vector.tensor_copy, (KEPT - 2) % 2)
            turn_tiles(dve, loop_use, LOOPS - 1, range(CUTS, 2 * CUTS - 2))
            dve.wait_ge(tiles_used, KEPT * CUTS - 3)
            dve.wait_ge(end_loaded[0], 64)
            turn_tile(RING - 2, turned[0], [0])
            dve.wait_ge(tiles_loaded[RING - 2], (loop_use.rounds + 2 * LOOPS) * 64)
            turn_tile(RING - 2, turned[0], [1])
            turn_end(dve, loop_use)
            sum_end(dve)

            done = [0, 0]

            def end_step(h, ins):
                done[h] += 1
                ins.then_inc(end_steps[h], 1)

            def end_stats_of(h, src, n):
                if done[h]:
                    dve.wait_ge(end_steps[h], done[h])
                for t in (2 * h, 2 * h + 1):
                    stats = nc.vector.bn_stats(end_stats[:, t, :], src(t))
                end_step(h, stats)
                dve.wait_ge(end_steps[h], done[h])
                for t in (2 * h, 2 * h + 1):
                    mv = nc.vector.bn_aggr(end_mv[:, t, :], end_stats[:, t, :])
                end_step(h, mv)
                dve.wait_ge(end_steps[h], done[h])
                end_step(h, nc.vector.tensor_scalar(end_var[:, 2 * h:2 * h + 2], end_mv[:, 2 * h:2 * h + 2, 1],
                                                    LN_EPS, None, ALU.add))
                assert done[h] == END_VAR[n]

            def end_norm(h, src, dst):
                done[h] += 1
                dve.wait_ge(end_steps[h], done[h])
                for t in (2 * h, 2 * h + 1):
                    y = nc.vector.tensor_scalar(dst(t), src(t), end_mv[:, t, 0:1], end_rstd[:, t:t + 1],
                                                ALU.subtract, ALU.mult)
                end_step(h, y)

            def end_affine(h):
                for t in (2 * h, 2 * h + 1):
                    centered = nc.vector.scalar_tensor_tensor(end_y[:, t, :], nat_of(t), end_mv[:, t, 0:1],
                                                              gamma_sb[:, :], ALU.subtract, ALU.mult)
                end_step(h, centered)
                done[h] += 1
                dve.wait_ge(end_steps[h], done[h])
                for t in (2 * h, 2 * h + 1):
                    y = nc.vector.scalar_tensor_tensor(end_y[:, t, :], end_y[:, t, :], end_rstd[:, t:t + 1],
                                                       end_add[:, t, :], ALU.mult, ALU.add)
                end_step(h, y)

            def nat_of(t):
                return end_nat[t // 2][:, D * (t % 2):D * (t % 2) + D]

            def y_of(t):
                return end_y[:, t, :]

            def x1_of(t):
                return x_all[:, (KEPT - 1) * TPG + t, :]

            dve.wait_ge(end_closed, 1)
            end_stats_of(0, nat_of, 0)
            dve.wait_ge(nat_ready, GROUPS)
            end_stats_of(1, nat_of, 0)
            dve.wait_ge(add_made, 2)
            for h in range(2):
                end_affine(h)
                end_stats_of(h, y_of, 1)
            dve.sem_inc(nat_read, 1)
            for h in range(2):
                end_norm(h, y_of, x1_of)
                end_stats_of(h, x1_of, 2)
            for h in range(2):
                end_norm(h, x1_of, y_of)
                assert done[h] == END_STEPS
            with dve.If(edges_may_survive(dve) > 0):
                message_dve(dve)

        @block.tensor
        def _(pe):
            pe.sem_inc(nat_read, 2)
            pe.wait_ge(x_loaded, 16)
            pe.wait_ge(const_made, 3)

            def turn_pairs(b):
                if b >= 4:
                    pe.wait_ge(pairs_copied, b - 3)
                for j in range(4):
                    t = 8 * b + 2 * j
                    mm = pe.transpose(bank[b % 4][:, P * j:P * j + P],
                                      x_all[:, t:t + 2, :].rearrange("p t d -> p (t d)"), ident[:, :])
                mm.then_inc(pairs_turned, 1)

            for b in range(4):
                turn_pairs(b)
            pe.wait_ge(const_loaded, 16 * 4)
            for b in range(BANKS):
                pe.wait_ge(pairs_copied, b + 1)
                if b >= 2:
                    pe.wait_ge(e_scaled, b - 1)
                for t in range(8 * b, 8 * b + 8):
                    odd, k = t % 2, 0 if t < USER_TILES else 1
                    mm = pe.matmul(xw_out(b, odd)[:, t % 8 // 2, :], xt_pairs[half(odd), P * (t // 2):P * (t // 2) + P],
                                   w_ui_sb[half(odd), D * k:D * k + D], start=True, stop=True)
                mm.then_inc(xw_done, 1)
                if b == 0:
                    turn_pairs(4)
            pe.wait_ge(e_made, BANKS)
            multiply_rows(pe, L0, 0, first=True)
            with pe.Fori(1, T // RING) as it:
                multiply_rows(pe, L0, it)
            pe.wait_ge(cols_copied, 2)
            for b in range(BANKS):
                turn_cols(pe, b, bank[b])
            pe.wait_ge(cols_made, BANKS)
            for n in range(LOOPED * CUTS):
                g, q = n // CUTS, n % CUTS
                multiply_tile(pe, n, g % 2, q)
                if q == 0 and g:
                    close_group(pe, g - 1, (g - 1) % 2, (g - 1) % 2, stack[:, :])
                if n == 2:
                    pe.wait_ge(cols_nat_ready, 1)
                if 2 <= n <= EARLY:
                    multiply_flipped(pe, n - 1)
                if n < EARLY:
                    flip_blocks(pe, n)
                if n == EARLY + 1:
                    close_group(pe, RING, 0, 0, stack[:, :])
            with pe.Fori(0, LOOPS - 1) as it:
                multiply_tiles(pe, loop_use, it, stack[:, :], 0)
            multiply_tiles(pe, loop_use, LOOPS - 1, stack[:, :], 0, range(CUTS))
            close_group(pe, GROUPS - 2, (KEPT - 2) % 2, GROUPS % 2, stack[:, :])
            for q in range(CUTS - 1):
                multiply_tile(pe, (KEPT - 1) * CUTS + q, END_K, q, last=CUTS - 2)
            multiply_end(pe)
            close_end(pe, stack[:, :])
            with pe.If(edges_may_survive(pe) > 0):
                message_pe(pe)


_INS = ("x", "adj", "w_ui", "diag", "par", "gamma", "beta", "w_qv", "w_q", "theta", "b_q", "b_v")


def kernel(**inputs):
    import numpy as np
    import concourse.bacc as bacc
    from concourse.bass_utils import run_bass_kernel_spmd as run

    a = {k: np.asarray(v) for k, v in inputs.items()}
    laid = {
        "x": a["x"],
        "adj": a["adj"],
        "w_ui": np.concatenate([a["L0_gnn_W_u"], a["L0_gnn_W_i"]], axis=1),
        "diag": np.ascontiguousarray(np.concatenate([a["L0_gnn_diag_u"], a["L0_gnn_diag_i"]]).reshape(-1, 128).T),
        "par": np.concatenate([a["L0_gnn_par_u"], a["L0_gnn_par_i"]]),
        "gamma": a["L0_gnn_ln_gamma"],
        "beta": a["L0_gnn_ln_beta"],
        "w_qv": np.concatenate([a["L1_gnn_W"], a["L1_gnn_Wv"]], axis=1),
        "w_q": a["L1_gnn_Wq"],
        "theta": a["L1_gnn_Theta"],
        "b_q": a["L1_gnn_bq"].reshape(-1, 1),
        "b_v": a["L1_gnn_bv"],
    }
    nc = bacc.Bacc("TRN2", target_bir_lowering=False, num_devices=1)
    arrays, args = {}, []
    for name in _INS:
        v = np.ascontiguousarray(laid[name])
        arrays[f"in_{name}"] = v
        args.append(nc.dram_tensor(f"in_{name}", v.shape, mybir.dt.from_np(v.dtype), kind="ExternalInput").ap())
    shape = a["x"].shape
    args.append(nc.dram_tensor("out_0", shape, mybir.dt.from_np(a["x"].dtype), kind="ExternalOutput").ap())
    adjacency_layers_kernel(nc, *args)
    r = run(nc, [arrays], core_ids=[0])
    return r.results[0]["out_0"]
```
